# Optimizing a Trainium2 kernel written in Bass

```python
import numpy as np
import jax
import jax.numpy as jnp

def _softmax(x, axis=-1):
    return jax.nn.softmax(x, axis=axis)

def _gelu(x):
    return jax.nn.gelu(x, approximate=True)

def _silu(x):
    return jax.nn.silu(x)

def _sigmoid(x):
    return jax.nn.sigmoid(x)

def _layernorm(x, axis=-1, eps=1e-05):
    m = jnp.mean(x, axis=axis, keepdims=True)
    v = jnp.var(x, axis=axis, keepdims=True)
    return (x - m) / jnp.sqrt(v + eps)

def _scatter_add(tgt, idx, src, axis=0):
    return tgt.at[idx].add(src)

def _segment_sum(src, seg, n):
    return jax.ops.segment_sum(src, seg, n)
kernel_name = 'mk_adj_resnorm_d4_adj_r2_c4e033'

def setup_inputs(seed: int=0):
    np.random.seed(seed)
    _w = jnp.asarray

    def _rec_inputs():
        import jax
        import jax.numpy as jnp
        _gk = jax.random.key(seed)
        x = -0.0005207 + 1.001 * jax.random.normal(jax.random.fold_in(_gk, 1), (4096, 128), jnp.float32)
        _a = jax.random.bernoulli(jax.random.fold_in(_gk, 2), 0.000488281, (4096, 4096))
        _a = jnp.logical_or(_a, jnp.eye(4096, dtype=bool))
        _af = _a.astype(jnp.float32)
        _af = _af * jax.random.uniform(jax.random.fold_in(_gk, 3), (4096, 4096), jnp.float32, 0.05, 1)
        adj = _af
        return (x, adj)
    x, adj = _rec_inputs()

    def _L0_gnn_setup():
        import jax, jax.numpy as jnp
        import numpy as np
        N = 4096
        D = 128
        L = 3

        def _cxin_conv(x, a, eps, W, b):
            ax = a @ x
            h = ax + (1.0 + eps[0]) * ax
            for i in range(L):
                h = jax.nn.relu(h @ W[i].T + b[i])
            return h
        key = jax.random.key(seed)
        ks = jax.random.split(key, 8)
        s = 1.0 / np.sqrt(D)
        return {'x1': jax.random.normal(ks[0], (N, D), jnp.float32), 'x2': jax.random.normal(ks[1], (N, D), jnp.float32), 'G1': jax.random.uniform(ks[2], (N, N), jnp.float32), 'G2': jax.random.uniform(ks[3], (N, N), jnp.float32), 'eps1': jnp.zeros((1,), jnp.float32), 'eps2': jnp.zeros((1,), jnp.float32), 'W1': jax.random.normal(ks[4], (L, D, D), jnp.float32) * s, 'b1': jnp.zeros((L, D), jnp.float32), 'W2': jax.random.normal(ks[5], (L, D, D), jnp.float32) * s, 'b2': jnp.zeros((L, D), jnp.float32), 'Wm': jax.random.normal(ks[6], (D, 2 * D), jnp.float32) * (1.0 / np.sqrt(2 * D)), 'bm': jnp.zeros((D,), jnp.float32)}
    _L0_gnn_all = _L0_gnn_setup()
    _L0_gnn_in = {k: v for k, v in _L0_gnn_all.items() if k in ('x2', 'eps1', 'eps2', 'W1', 'b1', 'W2', 'b2', 'Wm', 'bm')}
    del _L0_gnn_all

    def _L1_gnn_setup():
        import jax, jax.numpy as jnp
        import numpy as np
        MIN_NORM = 1e-15
        BALL_EPS = 1e-05
        C_IN = 1.0
        C_OUT = 1.0

        def _artanh(x):
            x = jnp.clip(x, -1.0 + 1e-07, 1.0 - 1e-07)
            return 0.5 * (jnp.log1p(x) - jnp.log1p(-x))

        def _norm(x):
            return jnp.maximum(jnp.linalg.norm(x, axis=-1, keepdims=True), MIN_NORM)

        def proj(x, c):
            norm = _norm(x)
            maxnorm = (1.0 - BALL_EPS) / jnp.sqrt(c)
            return jnp.where(norm > maxnorm, x / norm * maxnorm, x)

        def expmap0(u, c):
            sc = jnp.sqrt(c)
            un = _norm(u)
            return jnp.tanh(sc * un) * u / (sc * un)

        def logmap0(p, c):
            sc = jnp.sqrt(c)
            pn = _norm(p)
            return _artanh(sc * pn) * p / (sc * pn)

        def mobius_matvec(m, x, c):
            sc = jnp.sqrt(c)
            xn = _norm(x)
            mx = x @ m.T
            mxn = _norm(mx)
            res = jnp.tanh(mxn / xn * _artanh(sc * xn)) * mx / (mxn * sc)
            zero_row = jnp.all(mx == 0, axis=-1, keepdims=True)
            return jnp.where(zero_row, jnp.zeros((), dtype=res.dtype), res)

        def mobius_add(x, y, c):
            x2 = jnp.sum(x * x, axis=-1, keepdims=True)
            y2 = jnp.sum(y * y, axis=-1, keepdims=True)
            xy = jnp.sum(x * y, axis=-1, keepdims=True)
            num = (1.0 + 2.0 * c * xy + c * y2) * x + (1.0 - c * x2) * y
            denom = 1.0 + 2.0 * c * xy + c * c * x2 * y2
            return num / jnp.maximum(denom, MIN_NORM)
        key = jax.random.key(seed)
        k1, k2, k3, k4 = jax.random.split(key, 4)
        N, D_IN, D_OUT = (4096, 128, 128)
        x = proj(0.05 * jax.random.normal(k1, (N, D_IN), dtype=jnp.float32), C_IN)
        adj = jax.random.uniform(k2, (N, N), dtype=jnp.float32)
        adj = adj / jnp.sum(adj, axis=1, keepdims=True)
        bound = np.sqrt(2.0) * np.sqrt(6.0 / (D_IN + D_OUT))
        weight = jax.random.uniform(k3, (D_OUT, D_IN), dtype=jnp.float32, minval=-bound, maxval=bound)
        bias = 0.01 * jax.random.normal(k4, (D_OUT,), dtype=jnp.float32)
        return {'x': x, 'adj': adj, 'weight': weight, 'bias': bias}
    _L1_gnn_all = _L1_gnn_setup()
    _L1_gnn_in = {k: v for k, v in _L1_gnn_all.items() if k in ('weight', 'bias')}
    del _L1_gnn_all

    def _L2_gnn_setup():
        import jax, jax.numpy as jnp
        import numpy as np
        N = 4096
        F = 128
        NEG_INF = -9000000000000000.0
        ALPHA = 0.2
        THRESH = 1e-06
        key = jax.random.key(seed)
        k1, k2, k3, k4 = jax.random.split(key, 4)
        x = jax.random.normal(k1, (N, F), jnp.float32)
        h0 = jax.random.normal(k2, (N, F), jnp.float32)
        limit = float(np.sqrt(6.0 / (2 * F + 1)) * 1.414)
        a = jax.random.uniform(k3, (2 * F, 1), jnp.float32, -limit, limit)
        temp = jnp.zeros((5,), jnp.float32)
        adj = jax.random.bernoulli(k4, 0.005, (N, N)).astype(jnp.float32)
        adj = jnp.maximum(adj, jnp.eye(N, dtype=jnp.float32))
        return {'x': x, 'h0': h0, 'a': a, 'temp': temp, 'adj': adj, 'l': 1}
    _L2_gnn_all = _L2_gnn_setup()
    _L2_gnn_in = {k: v for k, v in _L2_gnn_all.items() if k in ('h0', 'a', 'temp')}
    del _L2_gnn_all

    def _L3_gnn_setup():
        import jax, jax.numpy as jnp
        import numpy as np
        N = 4096
        IN_DIM = 128
        OUT_DIM = 128
        ALPHA = 0.2
        NEG_INF = -9000000000000000.0
        key = jax.random.key(seed)
        k_h, k_w, k_a, k_adj = jax.random.split(key, 4)
        h = jax.random.normal(k_h, (N, IN_DIM), dtype=jnp.float32)
        w_bound = float(np.sqrt(6.0 / (IN_DIM + OUT_DIM)))
        W = jax.random.uniform(k_w, (IN_DIM, OUT_DIM), dtype=jnp.float32, minval=-w_bound, maxval=w_bound)
        a_bound = float(np.sqrt(6.0 / (2 * OUT_DIM + 1)))
        a = jax.random.uniform(k_a, (2 * OUT_DIM, 1), dtype=jnp.float32, minval=-a_bound, maxval=a_bound)
        adj = (jax.random.uniform(k_adj, (N, N), dtype=jnp.float32) < 0.01).astype(jnp.float32)
        adj = jnp.maximum(adj, jnp.eye(N, dtype=jnp.float32))
        return {'h': h, 'adj': adj, 'W': W, 'a': a}
    _L3_gnn_all = _L3_gnn_setup()
    _L3_gnn_in = {k: v for k, v in _L3_gnn_all.items() if k in ('W', 'a')}
    del _L3_gnn_all
    return {'x': x, 'adj': adj, 'L0_gnn_x2': _L0_gnn_in['x2'], 'L0_gnn_eps1': _L0_gnn_in['eps1'], 'L0_gnn_eps2': _L0_gnn_in['eps2'], 'L0_gnn_W1': _L0_gnn_in['W1'], 'L0_gnn_b1': _L0_gnn_in['b1'], 'L0_gnn_W2': _L0_gnn_in['W2'], 'L0_gnn_b2': _L0_gnn_in['b2'], 'L0_gnn_Wm': _L0_gnn_in['Wm'], 'L0_gnn_bm': _L0_gnn_in['bm'], 'L1_gnn_weight': _L1_gnn_in['weight'], 'L1_gnn_bias': _L1_gnn_in['bias'], 'L2_gnn_h0': _L2_gnn_in['h0'], 'L2_gnn_a': _L2_gnn_in['a'], 'L2_gnn_temp': _L2_gnn_in['temp'], 'L3_gnn_W': _L3_gnn_in['W'], 'L3_gnn_a': _L3_gnn_in['a']}

def reference(x, adj, L0_gnn_x2, L0_gnn_eps1, L0_gnn_eps2, L0_gnn_W1, L0_gnn_b1, L0_gnn_W2, L0_gnn_b2, L0_gnn_Wm, L0_gnn_bm, L1_gnn_weight, L1_gnn_bias, L2_gnn_h0, L2_gnn_a, L2_gnn_temp, L3_gnn_W, L3_gnn_a):
    import jax
    import jax.numpy as jnp

    def _L0_gnn_ref(x1, x2, G1, G2, eps1, eps2, W1, b1, W2, b2, Wm, bm):
        import jax, jax.numpy as jnp
        import numpy as np
        N = 4096
        D = 128
        L = 3

        def _cxin_conv(x, a, eps, W, b):
            ax = a @ x
            h = ax + (1.0 + eps[0]) * ax
            for i in range(L):
                h = jax.nn.relu(h @ W[i].T + b[i])
            return h
        out1 = _cxin_conv(x1, G1, eps1, W1, b1)
        out2 = _cxin_conv(x2, G2, eps2, W2, b2)
        merged = jnp.concatenate((out1, out2), axis=1)
        return merged @ Wm.T + bm

    def _L1_gnn_ref(x, adj, weight, bias):
        import jax, jax.numpy as jnp
        import numpy as np
        MIN_NORM = 1e-15
        BALL_EPS = 1e-05
        C_IN = 1.0
        C_OUT = 1.0

        def _artanh(x):
            x = jnp.clip(x, -1.0 + 1e-07, 1.0 - 1e-07)
            return 0.5 * (jnp.log1p(x) - jnp.log1p(-x))

        def _norm(x):
            return jnp.maximum(jnp.linalg.norm(x, axis=-1, keepdims=True), MIN_NORM)

        def proj(x, c):
            norm = _norm(x)
            maxnorm = (1.0 - BALL_EPS) / jnp.sqrt(c)
            return jnp.where(norm > maxnorm, x / norm * maxnorm, x)

        def expmap0(u, c):
            sc = jnp.sqrt(c)
            un = _norm(u)
            return jnp.tanh(sc * un) * u / (sc * un)

        def logmap0(p, c):
            sc = jnp.sqrt(c)
            pn = _norm(p)
            return _artanh(sc * pn) * p / (sc * pn)

        def mobius_matvec(m, x, c):
            sc = jnp.sqrt(c)
            xn = _norm(x)
            mx = x @ m.T
            mxn = _norm(mx)
            res = jnp.tanh(mxn / xn * _artanh(sc * xn)) * mx / (mxn * sc)
            zero_row = jnp.all(mx == 0, axis=-1, keepdims=True)
            return jnp.where(zero_row, jnp.zeros((), dtype=res.dtype), res)

        def mobius_add(x, y, c):
            x2 = jnp.sum(x * x, axis=-1, keepdims=True)
            y2 = jnp.sum(y * y, axis=-1, keepdims=True)
            xy = jnp.sum(x * y, axis=-1, keepdims=True)
            num = (1.0 + 2.0 * c * xy + c * y2) * x + (1.0 - c * x2) * y
            denom = 1.0 + 2.0 * c * xy + c * c * x2 * y2
            return num / jnp.maximum(denom, MIN_NORM)
        h = proj(mobius_matvec(weight, x, C_IN), C_IN)
        hyp_bias = proj(expmap0(bias[None, :], C_IN), C_IN)
        h = proj(mobius_add(h, hyp_bias, C_IN), C_IN)
        x_tangent = logmap0(h, C_IN)
        support_t = adj @ x_tangent
        h = proj(expmap0(support_t, C_IN), C_IN)
        xt = jax.nn.relu(logmap0(h, C_IN))
        return proj(expmap0(xt, C_OUT), C_OUT)

    def _L2_gnn_ref(x, h0, a, temp, adj, l):
        import jax, jax.numpy as jnp
        import numpy as np
        N = 4096
        F = 128
        NEG_INF = -9000000000000000.0
        ALPHA = 0.2
        THRESH = 1e-06
        Fdim = x.shape[1]
        feat_1 = x @ a[:Fdim]
        feat_2 = x @ a[Fdim:]
        e = jax.nn.leaky_relu(feat_1 + feat_2.T, ALPHA)
        att = jnp.where(adj > 0, e, NEG_INF)
        U = jax.nn.softmax(att, axis=1)
        P = 0.5 * U
        prop_u = U @ x
        rowsum = jnp.sum(U * P, axis=1)
        coe = jax.nn.sigmoid(temp)
        xi = x * rowsum[:, None]
        feat_odd = prop_u - xi
        feat_even = x + prop_u - xi
        feat = coe[2] * feat_odd + (1.0 - coe[2]) * feat_even
        sgn = jnp.sign(feat)
        mod = jnp.abs(feat)
        mod = jnp.where(mod > THRESH, mod - THRESH, 0.0)
        feat = mod * sgn
        pu = U @ feat
        feat_odd2 = feat - coe[3] * pu
        feat_even2 = pu + feat_odd2 * rowsum[:, None]
        feat_odd2 = coe[0] * feat_odd2 + (1.0 - coe[0]) * h0
        out = coe[1] * feat_even2 + (1.0 - coe[1]) * feat_odd2
        return out

    def _L3_gnn_ref(h, adj, W, a):
        import jax, jax.numpy as jnp
        import numpy as np
        N = 4096
        IN_DIM = 128
        OUT_DIM = 128
        ALPHA = 0.2
        NEG_INF = -9000000000000000.0
        Wh = h @ W
        Wh1 = Wh @ a[:OUT_DIM, :]
        Wh2 = Wh @ a[OUT_DIM:, :]
        e = jax.nn.leaky_relu(Wh1 + Wh2.T, negative_slope=ALPHA)
        attention = jax.nn.softmax(jnp.where(adj > 0, e, NEG_INF), axis=1)
        h_prime = attention @ Wh
        return jax.nn.elu(h_prime)
    x = _layernorm(x + _L0_gnn_ref(x, L0_gnn_x2, adj, adj, L0_gnn_eps1, L0_gnn_eps2, L0_gnn_W1, L0_gnn_b1, L0_gnn_W2, L0_gnn_b2, L0_gnn_Wm, L0_gnn_bm), axis=-1)
    x = _layernorm(x + _L1_gnn_ref(x, adj, L1_gnn_weight, L1_gnn_bias), axis=-1)
    x = _layernorm(x + _L2_gnn_ref(x, L2_gnn_h0, L2_gnn_a, L2_gnn_temp, adj, 1), axis=-1)
    x = _layernorm(x + _L3_gnn_ref(x, adj, L3_gnn_W, L3_gnn_a), axis=-1)
    return x

_drawn_inputs = setup_inputs


def setup_inputs(seed=0):
    import zlib

    import numpy as np

    out = dict(_drawn_inputs(seed))
    spreads = {'L0_gnn_b1': (0.0, 0.1),
     'L0_gnn_b2': (0.0, 0.1),
     'L0_gnn_bm': (0.0, 0.1),
     'L2_gnn_temp': (0.0, 2.0)}
    factors = {'L1_gnn_bias': 64.0}
    for name, (base, spread) in spreads.items():
        noise = np.random.default_rng([zlib.crc32(name.encode()), seed]).standard_normal(out[name].shape)
        drawn = base * np.exp(spread * noise) if base else spread * noise
        out[name] = jnp.asarray(drawn.astype(out[name].dtype))
    for name, factor in factors.items():
        out[name] = (out[name] * factor).astype(out[name].dtype)
    return out
```

```python
from contextlib import ExitStack

import concourse.bass as bass
from concourse import mybir

F32 = mybir.dt.float32
BF16 = mybir.dt.bfloat16
U8 = mybir.dt.uint8
ALU = mybir.AluOpType
ACT = mybir.ActivationFunctionType
AX = mybir.AxisListType.X
RMAX = bass.bass_isa.ReduceOp.max
ds = bass.ds

P = 128
N = 4096
D = 128
NB = N // P
NG = 8
GB = NB // NG
GC = GB * P
YW = D + 1
LAYERS = 3
SETUP_STEPS, L0_STEPS, L1_STEPS, P2_STEPS, L2A_STEPS, L2B_STEPS, P3_STEPS, L3_STEPS = 8, 56, 21, 17, 13, 11, 8, 12
ARENA = 53208

MIN_NORM = 1e-15
MAX_NORM = 1.0 - 1e-5
CLIP = 1.0 - 1e-7
LN_EPS = 1e-5
SLOPE = 0.2
THRESH = 1e-6
ARTANH_MAX = 6.1023553


def build(nc, t):
    ctx = ExitStack()
    with ctx:
        def sem(name):
            return ctx.enter_context(nc.semaphore(name))

        arena = ctx.enter_context(nc.sbuf_tensor("arena", [P, ARENA], F32))
        used = [0]

        def take(words):
            a = used[0]
            used[0] += words
            assert used[0] <= ARENA, used
            return arena[:, a:a + words]

        def blocks(ap, w=D):
            return ap.rearrange("p (b d) -> p b d", d=w)

        mask_words = take(N * NB // 4)
        mask = mask_words.bitcast(U8).rearrange("p (b i) -> p b i", i=N)
        nodes = blocks(take(NB * D))
        y_words = take(NB * YW)
        tangent = blocks(y_words[:, 0:NB * D])
        y = blocks(y_words, YW)
        yfeat_words = take(NB * D)
        yfeat = blocks(yfeat_words)
        ring = take(4096)
        adj_ring1 = ring.rearrange("p (s b i) -> p s b i", s=4, i=GC)
        w_ring = ring[:, 0:4 * GC].rearrange("p (s i) -> p s i", s=4)
        over_ring = ring[:, 2048:3072].bitcast(BF16).rearrange("p (s i) -> p s i", s=4)
        edge_ring = ring[:, 3072:4096].bitcast(BF16).rearrange("p (s i) -> p s i", s=4)
        g_now = take(GC)
        g_next = take(GC)
        num = blocks(take(GB * YW), YW)
        t1, t2, t4 = [blocks(take(GC)) for _ in range(3)]
        ident = take(P)
        ones = take(1)
        w3 = take(D)
        avec3 = take(2 * D)
        sqs = take(NB * 3).bitcast(BF16).rearrange("p (b s) -> p b s", s=6)
        f1, f2, bcol, kcol, gcol, gsq = [take(NB) for _ in range(6)]
        rgam = gsq
        coe = take(5)
        st = take(GB * 6).rearrange("p (b s) -> p b s", s=6)
        mv = take(GB * 2).rearrange("p (b s) -> p b s", s=2)
        c = [take(GB) for _ in range(8)]
        roots = take(2 * GB)
        qsum = take(GB * 9)
        q3 = take(GB * 3).rearrange("p (b s) -> p b s", s=3)
        pair, pairmax = take(2), take(2)
        sc = take(12)
        spare = take(1)
        y2, nbsq, nbn, nbt, om2, oc0, kap, nc3 = [sc[:, i:i + 1] for i in range(8)]
        half_range, neg_mid, beta, g_low = [sc[:, i:i + 1] for i in range(8, 12)]

        over = [0]

        def early(words):
            a = over[0]
            over[0] += words
            assert over[0] <= N * NB // 4
            return mask_words[:, a:a + words]

        x1in = blocks(early(NB * D))
        x2in = blocks(early(NB * D))
        adj_ring0 = early(8192).rearrange("p (s b i) -> p s b i", s=4, i=GC)
        w1t = early(LAYERS * D)
        w2t = early(LAYERS * D)
        wmt = early(2 * D)
        whyp = early(D)
        bm = early(D)
        hb = early(D)
        b1, b2 = early(LAYERS), early(LAYERS)
        epsc = early(2)
        ha = [early(GC) for _ in range(2)]
        hbb = [early(GC) for _ in range(2)]
        mx, e2, e3, norm0 = [blocks(early(GC)) for _ in range(4)]
        turned0 = early(GC)
        avec2 = yfeat_words[:, 0:2 * D]
        sums_t = yfeat_words[:, 2 * D:2 * D + GC]
        norm2 = blocks(ring[:, 2048:2560])
        turned2 = ring[:, 2560:3072]
        N_INPUTS = 16

        def bank(name):
            return ctx.enter_context(nc.psum_tensor(name, [P, 512], F32))

        sum_a, sum_b = bank("sum_a"), bank("sum_b")
        mlp_a, mlp_b = bank("mlp_a"), bank("mlp_b")
        rows_ps = bank("rows_ps")
        turn_ps = bank("turn_ps")
        map_ps = bank("map_ps")
        g_ps = bank("g_ps")
        sq_ps = mlp_a

        inputs_in = sem("inputs_in")
        adj_in = [sem(f"adj_in{s}") for s in range(4)]
        h0_in = sem("h0_in")
        out_written = sem("out_written")
        adj_used = sem("adj_used")
        adj_used1 = sem("adj_used1")
        mask_made = sem("mask_made")
        ident_made = sem("ident_made")
        setup_done = sem("setup_done")
        sums_copied = sem("sums_copied")
        mlp_in = sem("mlp_in")
        mlp_out = sem("mlp_out")
        merged = sem("merged")
        rows_normed = sem("rows_normed")
        rows_saved = sem("rows_saved")
        turned = sem("turned")
        turned_copied = sem("turned_copied")
        mapped = sem("mapped")
        mapped_copied = sem("mapped_copied")
        ask = sem("ask")
        answer = sem("answer")
        dve_step = sem("dve_step")
        tangent_made = sem("tangent_made")
        layer_ready = sem("layer_ready")
        feat_done = sem("feat_done")
        range_asked = sem("range_asked")
        range_known = sem("range_known")
        diag_made = sem("diag_made")
        g_spread = sem("g_spread")
        g_fetched = sem("g_fetched")
        g_taken = sem("g_taken")
        w_made = sem("w_made")
        over_made = sem("over_made")
        edge_made = sem("edge_made")
        w_used = sem("w_used")

        block = ctx.enter_context(nc.Block())

        def group(ap, g):
            return ap[:, ds(4 * g, GB), :]

        def gcols(ap, g):
            return ap[:, ds(4 * g, GB)]

        def wide(col, w=D):
            return col.rearrange("p (b o) -> p b o", o=1).to_broadcast([P, GB, w])

        def flat(t3):
            return t3.rearrange("p b d -> p (b d)")

        CH0, CH1 = 4, 2
        NC0, NC1 = NB // CH0, NB // CH1
        LAPS0 = NG * NC0 // 4
        LOADS0 = NG * NC0

        ASK0, ASK1, ASK3, ASK4 = 6, 4, 1, 2
        PREP = 1
        A_L0 = 2
        A_L1 = A_L0 + NG * ASK0
        A_P2 = A_L1 + NG * ASK1
        A_L2B = A_P2 + PREP
        A_P3 = A_L2B + NG * ASK3
        A_L3 = A_P3 + PREP

        @block.sync
        def _(sp):
            def small(dst, src):
                sp.dma_start(dst, src).then_inc(inputs_in, 16)

            small(x1in, t["x"].rearrange("(b p) d -> p b d", p=P))
            small(x2in, t["L0_gnn_x2"].rearrange("(b p) d -> p b d", p=P))
            small(w1t, t["L0_gnn_W1t"].rearrange("l d e -> d l e"))
            small(w2t, t["L0_gnn_W2t"].rearrange("l d e -> d l e"))
            small(wmt, t["L0_gnn_Wmt"].rearrange("(l d) e -> d l e", l=2))
            small(whyp, t["L1_gnn_weight_t"])
            small(bm, t["L0_gnn_bm"].rearrange("(a d) -> a d", a=1).to_broadcast([P, D]))
            small(hb, t["L1_gnn_bias"].rearrange("(a d) -> a d", a=1).to_broadcast([P, D]))
            small(b1, t["L0_gnn_b1t"])
            small(b2, t["L0_gnn_b2t"])
            small(epsc[:, 0:1], t["L0_gnn_eps1"].rearrange("(a d) -> a d", a=1).to_broadcast([P, 1]))
            small(epsc[:, 1:2], t["L0_gnn_eps2"].rearrange("(a d) -> a d", a=1).to_broadcast([P, 1]))
            small(coe, t["L2_gnn_temp"].rearrange("(a d) -> a d", a=1).to_broadcast([P, 5]))
            small(w3, t["L3_gnn_W"])
            small(avec2, t["L2_gnn_a"].rearrange("d a -> a d").to_broadcast([P, 2 * D]))
            small(avec3, t["L3_gnn_a"].rearrange("d a -> a d").to_broadcast([P, 2 * D]))

            adj = t["adj_t"]

            def load0(g, c):
                src = adj[ds(g, 1), :, ds(c * CH0 * GC, CH0 * GC)].rearrange("a p n -> (a p) n")
                sp.dma_start(adj_ring0[:, c % 4].rearrange("p b i -> p (b i)"), src).then_inc(adj_in[c % 4], 16)

            def load1(g, c):
                src = adj[ds(g, 1), :, ds(c * CH1 * GC, CH1 * GC)].rearrange("a p n -> (a p) n")
                sp.dma_start(adj_ring1[:, c % 4].rearrange("p b i -> p (b i)"), src).then_inc(adj_in[c % 4], 16)

            for c in range(NC0):
                if c >= 4:
                    sp.wait_ge(adj_used, c - 3)
                load0(0, c)
            with sp.Fori(1, NG) as g:
                for c in range(NC0):
                    sp.wait_ge(adj_used, g * NC0 + (c - 3))
                    load0(g, c)
            for c in range(NC1):
                if c >= 4:
                    sp.wait_ge(adj_used1, c - 3)
                    sp.wait_ge(mask_made, c - 3)
                else:
                    sp.wait_ge(adj_used, LOADS0)
                load1(0, c)
            with sp.Fori(1, NG) as g:
                for c in range(NC1):
                    chunk = g * NC1 + (c - 3)
                    sp.wait_ge(adj_used1, chunk)
                    sp.wait_ge(mask_made, chunk)
                    load1(g, c)
            h0 = t["L2_gnn_h0"].rearrange("(b p) d -> p b d", p=P)
            sp.wait_ge(layer_ready, 1)
            sp.dma_start(t4, h0[:, 0:GB, :]).then_inc(h0_in, 16)
            with sp.Fori(1, NG) as g:
                sp.wait_ge(feat_done, g)
                sp.dma_start(t4, group(h0, g)).then_inc(h0_in, 16)
            out = t["out"].rearrange("(b p) d -> p b d", p=P)
            with sp.Fori(0, NG) as g:
                sp.wait_ge(rows_normed, g + (2 * NG + 1))
                sp.dma_start(group(out, g), norm2).then_inc(out_written, 16)
            sp.wait_ge(out_written, 16 * NG)

        @block.gpsimd
        def _(pool):
            nc.gpsimd.memset(ident, 0.0).then_inc(ident_made, 1)
            pool.wait_ge(ident_made, 1)
            nc.gpsimd.affine_select(out=ident, in_=ident, compare_op=ALU.not_equal, fill=1.0, base=0,
                                    pattern=[[-1, P]], channel_multiplier=1).then_inc(ident_made, 1)
            pool.wait_ge(ident_made, 2)

            def diag(g, n):
                if not isinstance(n, int) or n > 0:
                    pool.wait_ge(g_taken, n)
                nc.gpsimd.tensor_tensor(blocks(g_next), ident.rearrange("p (o d) -> p o d", o=1).to_broadcast([P, GB, D]),
                                        wide(gcols(gcol, g)), ALU.mult).then_inc(diag_made, 1)

            for lay in range(3):
                if lay != 1:
                    pool.wait_ge(range_asked, 1 if lay == 0 else 2)
                    nc.gpsimd.partition_all_reduce(pairmax, pair, P, RMAX).then_inc(range_known, 1)
                    pool.wait_ge(layer_ready, 1 if lay == 0 else 2)
                diag(0, lay * NG)
                with pool.Fori(1, NG) as g:
                    diag(g, g + lay * NG)

        @block.tensor
        def _(pe):
            def mm(out, w, m, start, stop, **kw):
                return nc.tensor.matmul(out, w, m, start=start, stop=stop, **kw)

            def turn(n, src):
                pe.wait_ge(rows_normed, n + 1)
                for b in range(GB):
                    last = nc.tensor.transpose(turn_ps[:, b * P:(b + 1) * P], src[:, b, :], ident)
                last.then_inc(turned, 1)

            pe.wait_ge(inputs_in, 16 * N_INPUTS)
            pe.wait_ge(ident_made, 2)

            def mlp_layer(g, l):
                pe.wait_ge(mlp_in, g * 8 + 2 * (l + 1))
                mm(mlp_a[:, :], w1t[:, l * D:(l + 1) * D], ha[l % 2], True, True)
                mm(mlp_b[:, :], w2t[:, l * D:(l + 1) * D], hbb[l % 2], True, True).then_inc(mlp_out, 1)

            def merge(g, first):
                pe.wait_ge(mlp_in, g * 8 + 8)
                if not first:
                    pe.wait_ge(rows_normed, g)
                for b in range(GB):
                    s = slice(b * P, (b + 1) * P)
                    mm(rows_ps[:, s], ha[1][:, s], wmt[:, 0:D], True, False)
                    last = mm(rows_ps[:, s], hbb[1][:, s], wmt[:, D:2 * D], False, True)
                last.then_inc(merged, 1)

            def hyp_map(g, first=0):
                pe.wait_ge(turned_copied, g + 1)
                for b in range(GB):
                    last = mm(map_ps[:, b * P:(b + 1) * P], turned0[:, b * P:(b + 1) * P], whyp, True, True)
                last.then_inc(mapped, 1)

            def l0_after(g, jb):
                if jb in (2, 6, 10):
                    mlp_layer(g, (jb - 2) // 4)
                if jb == 14:
                    merge(g, isinstance(g, int) and g == 0)
                if jb == 20:
                    turn(g, norm0)
                if jb == 23:
                    hyp_map(g)

            def l0_sums(g, prev=None):
                for jb in range(NB):
                    c, q = divmod(jb, CH0)
                    if q == 0:
                        pe.wait_ge(adj_in[c % 4], g * (16 * NC0 // 4) + 16 * (c // 4 + 1))
                    if jb == 0 and prev is not None:
                        pe.wait_ge(mlp_in, g * 8 - 6)
                    mm(sum_a[:, :], x1in[:, jb, :], adj_ring0[:, c % 4, q, :], jb == 0, jb == NB - 1)
                    last = mm(sum_b[:, :], x2in[:, jb, :], adj_ring0[:, c % 4, q, :], jb == 0, jb == NB - 1)
                    if q == CH0 - 1:
                        last.then_inc(adj_used, 1)
                    if prev is not None:
                        l0_after(prev, jb)

            l0_sums(0)
            with pe.Fori(1, NG) as g:
                l0_sums(g, g - 1)
            for jb in range(NB):
                l0_after(NG - 1, jb)

            pe.wait_ge(tangent_made, NG)

            def turn_back(g):
                pe.wait_ge(sums_copied, g + 1)
                for b in range(GB):
                    last = nc.tensor.transpose(rows_ps[:, b * P:(b + 1) * P], sums_t[:, b * P:(b + 1) * P], ident)
                last.then_inc(merged, 1)

            def l1_sums(g, prev=None):
                for jb in range(NB):
                    c, q = divmod(jb, CH1)
                    if q == 0:
                        pe.wait_ge(adj_in[c % 4], g * (16 * NC1 // 4) + 16 * (LAPS0 + c // 4 + 1))
                    if jb == 0 and prev is not None:
                        pe.wait_ge(sums_copied, g)
                    last = mm(sum_a[:, :], tangent[:, jb, :], adj_ring1[:, c % 4, q, :], jb == 0, jb == NB - 1)
                    if q == CH1 - 1:
                        last.then_inc(adj_used1, 1)
                    if prev is not None and jb == 2:
                        turn_back(prev)

            l1_sums(0)
            with pe.Fori(1, NG) as g:
                l1_sums(g, g - 1)
            turn_back(NG - 1)

            def spread(n):
                pe.wait_ge(diag_made, n + 1)
                if not isinstance(n, int) or n > 0:
                    pe.wait_ge(g_fetched, n)
                mm(g_ps[:, :], ones.to_broadcast([P, P]), g_next, True, True).then_inc(g_spread, 1)

            def weigh(lay, g, feats, width, prev, after):
                for jb in range(NB):
                    n = g * NB + lay * NG * NB + jb
                    s = jb % 4
                    if jb == 0 and prev is not None:
                        pe.wait_ge(sums_copied, g + (1 + lay) * NG)
                    elif jb == 0:
                        pe.wait_ge(sums_copied, (1 + lay) * NG)
                    pe.wait_ge(w_made, n + 1)
                    for b in range(GB):
                        ps = (sum_a, sum_b)[b // 2]
                        o = (b % 2) * YW
                        last = mm(ps[:, o:o + width], w_ring[:, s, b * P:(b + 1) * P], feats[:, jb, 0:width],
                                  jb == 0 and b % 2 == 0, jb == NB - 1, skip_group_check=True)
                    if lay == 0:
                        pe.wait_ge(over_made, n + 1)
                        for b in range(GB):
                            mm(sq_ps[:, b * 9:b * 9 + 6], over_ring[:, s, b * P:(b + 1) * P], sqs[:, jb, :],
                               jb == 0 and b == 0, jb == NB - 1, skip_group_check=True)
                        pe.wait_ge(edge_made, n + 1)
                        for b in range(GB):
                            last = mm(sq_ps[:, b * 9 + 6:b * 9 + 9], edge_ring[:, s, b * P:(b + 1) * P], sqs[:, jb, 3:6],
                                      False, jb == NB - 1, skip_group_check=True)
                    last.then_inc(w_used, 1)
                    if jb == 12:
                        last_group = isinstance(g, int) and g == NG - 1
                        if not last_group:
                            spread(g + (lay * NG + 1))
                    if prev is not None:
                        after(prev, jb)

            def nothing(g, jb):
                pass

            def wh_after(g, jb):
                if jb == 16:
                    turn(g + NG, norm2)
                if jb == 20:
                    pe.wait_ge(turned_copied, g + (NG + 1))
                    for b in range(GB):
                        last = mm(map_ps[:, b * P:(b + 1) * P], turned2[:, b * P:(b + 1) * P], w3, True, True)
                    last.then_inc(mapped, 1)

            for lay, feats, width, after in ((0, y, YW, nothing), (1, yfeat, D, wh_after), (2, y, YW, nothing)):
                if lay == 1:
                    pe.wait_ge(feat_done, NG)
                else:
                    pe.wait_ge(layer_ready, 1 if lay == 0 else 2)
                spread(lay * NG)
                weigh(lay, 0, feats, width, None, after)
                with pe.Fori(1, NG - 1) as g:
                    weigh(lay, g, feats, width, g - 1, after)
                weigh(lay, NG - 1, feats, width, NG - 2, after)
                for jb in range(NB):
                    after(NG - 1, jb)

        @block.scalar
        def _(act):
            def fn(out, in_, func, **kw):
                return nc.scalar.activation(out, in_, func, **kw)

            def on_ask(n, out, in_, func, **kw):
                act.wait_ge(ask, n + 1)
                fn(out, in_, func, **kw).then_inc(answer, 1)

            act.wait_ge(ask, 1)
            fn(coe, coe, ACT.Sigmoid)
            fn(nbn, nbsq, ACT.Sqrt).then_inc(answer, 1)
            on_ask(1, nbt, nbn, ACT.Tanh)
            act.wait_ge(setup_done, 1)

            def l0_rows(g, first=False):
                act.wait_ge(adj_used, g * NC0 + NC0)
                fn(ha[0], sum_a[:, :], ACT.Copy, scale=epsc[:, 0:1]).then_inc(mlp_in, 1)
                fn(hbb[0], sum_b[:, :], ACT.Copy, scale=epsc[:, 1:2]).then_inc(mlp_in, 1)
                for l in range(LAYERS):
                    act.wait_ge(mlp_out, g * LAYERS + (l + 1))
                    if l == 0 and not first:
                        act.wait_ge(merged, g)
                    fn(ha[(l + 1) % 2], mlp_a[:, :], ACT.Relu, bias=b1[:, l:l + 1]).then_inc(mlp_in, 1)
                    fn(hbb[(l + 1) % 2], mlp_b[:, :], ACT.Relu, bias=b2[:, l:l + 1]).then_inc(mlp_in, 1)
                n = g * ASK0 + A_L0
                on_ask(n, c[1], c[0], ACT.Sqrt)
                act.wait_ge(rows_normed, g + 1)
                fn(group(nodes, g), norm0, ACT.Copy).then_inc(rows_saved, 1)
                act.wait_ge(turned, g + 1)
                fn(turned0, turn_ps[:, :], ACT.Copy).then_inc(turned_copied, 1)
                act.wait_ge(mapped, g + 1)
                fn(flat(mx), map_ps[:, :], ACT.Copy).then_inc(mapped_copied, 1)
                on_ask(n + 1, roots, roots, ACT.Sqrt)
                on_ask(n + 2, c[3], c[1], ACT.Ln)
                on_ask(n + 3, c[1], c[0], ACT.Tanh)
                on_ask(n + 4, c[1], c[0], ACT.Sqrt)
                on_ask(n + 5, c[3], c[1], ACT.Ln)

            l0_rows(0, True)
            with act.Fori(1, NG) as g:
                l0_rows(g)

            def l1_rows(g):
                act.wait_ge(adj_used1, g * NC1 + NC1)
                fn(sums_t, sum_a[:, :], ACT.Copy).then_inc(sums_copied, 1)
                act.wait_ge(merged, g + (NG + 1))
                fn(flat(t1), rows_ps[:, :], ACT.Copy).then_inc(mapped_copied, 1)
                n = g * ASK1 + A_L1
                on_ask(n, c[1], c[0], ACT.Sqrt)
                on_ask(n + 1, c[1], c[0], ACT.Sqrt)
                on_ask(n + 2, c[4], c[1], ACT.Tanh)
                on_ask(n + 3, c[1], c[0], ACT.Sqrt)

            with act.Fori(0, NG) as g:
                l1_rows(g)

            def factors(n):
                act.wait_ge(ask, n + 1)
                fn(bcol, f2, ACT.Exp, bias=neg_mid)
                fn(kcol, f2, ACT.Exp, scale=-(1 - SLOPE), bias=beta)
                fn(gcol, gcol, ACT.Exp).then_inc(answer, 1)

            def fetch_g(n):
                act.wait_ge(g_spread, n + 1)
                fn(g_next, g_ps[:, :], ACT.Copy).then_inc(g_fetched, 1)

            def copy_sums(lay, g, width, first):
                act.wait_ge(w_used, g * NB + (lay * NG * NB + NB))
                if not first:
                    if lay == 0:
                        act.wait_ge(feat_done, g)
                    else:
                        act.wait_ge(rows_normed, g + lay * NG)
                for half, ps in enumerate((sum_a, sum_b)):
                    last = fn(num[:, 2 * half:2 * half + 2, 0:width],
                              ps[:, 0:2 * YW].rearrange("p (b d) -> p b d", d=YW)[:, :, 0:width], ACT.Copy)
                if lay == 0:
                    last = fn(qsum, sq_ps[:, 0:GB * 9], ACT.Copy)
                last.then_inc(sums_copied, 1)

            def edges(g, jb, first):
                n = g * NB + jb
                act.wait_ge(w_made, n + 1)
                if not first or jb >= 4:
                    act.wait_ge(w_used, n - 3)
                fn(edge_ring[:, jb % 4], w_ring[:, jb % 4], ACT.Sign).then_inc(edge_made, 1)

            factors(A_P2)
            fetch_g(0)

            def l2_first(g, first=False, last=False):
                for jb in range(NB):
                    edges(g, jb, first)
                    if jb == 16 and not last:
                        fetch_g(g + 1)
                copy_sums(0, g, YW, first)

            l2_first(0, first=True)
            with act.Fori(1, NG - 1) as g:
                l2_first(g)
            l2_first(NG - 1, last=True)

            def l2_second_rows(g):
                on_ask(g + A_L2B, c[1], c[0], ACT.Sqrt)
                act.wait_ge(rows_normed, g + (NG + 1))
                fn(group(nodes, g), norm2, ACT.Copy).then_inc(rows_saved, 1)
                return g

            def l2_second_maps(g):
                act.wait_ge(turned, g + (NG + 1))
                fn(turned2, turn_ps[:, :], ACT.Copy).then_inc(turned_copied, 1)
                act.wait_ge(mapped, g + (NG + 1))
                fn(group(y, g)[:, :, 0:D], blocks(map_ps[:, :]), ACT.Copy)
                fn(flat(t4), map_ps[:, :], ACT.Copy).then_inc(mapped_copied, 1)

            fetch_g(NG)
            fetch_g(NG + 1)
            copy_sums(1, 0, D, True)
            with act.Fori(1, NG - 1) as g:
                l2_second_rows(g - 1)
                fetch_g(g + (NG + 1))
                l2_second_maps(g - 1)
                copy_sums(1, g, D, False)
            l2_second_rows(NG - 2)
            l2_second_maps(NG - 2)
            copy_sums(1, NG - 1, D, False)
            l2_second_rows(NG - 1)
            l2_second_maps(NG - 1)

            def l3_rows(g):
                n = g * ASK4 + A_L3
                on_ask(n, flat(t4), flat(t2), ACT.Exp)
                on_ask(n + 1, c[1], c[0], ACT.Sqrt)

            factors(A_P3)
            fetch_g(2 * NG)
            fetch_g(2 * NG + 1)
            copy_sums(2, 0, YW, True)
            with act.Fori(1, NG - 1) as g:
                l3_rows(g - 1)
                fetch_g(g + (2 * NG + 1))
                copy_sums(2, g, YW, False)
            l3_rows(NG - 2)
            copy_sums(2, NG - 1, YW, False)
            l3_rows(NG - 1)

        @block.vector
        def _(dve):
            V = nc.vector
            tt, ts, stt = V.tensor_tensor, V.tensor_scalar, V.scalar_tensor_tensor
            base, count = [0], [0]

            def step(ins):
                count[0] += 1
                ins.then_inc(dve_step, 1)
                dve.wait_ge(dve_step, base[0] + count[0])

            def start(at):
                base[0], count[0] = at, 0

            def asks(ins):
                ins.then_inc(ask, 1)

            def answered(n):
                dve.wait_ge(answer, n + 1)

            def rowsum(out, in_):
                return V.tensor_reduce(out, in_, AX, ALU.add)

            def over_features(vec):
                return vec.rearrange("p (o d) -> p o d", o=1).to_broadcast([P, GB, D])

            def norm_stats(src):
                for b in range(GB):
                    last = V.bn_stats(st[:, b, :], src[:, b, :])
                step(last)
                V.memset(spare, 0.0)
                for b in range(GB):
                    last = V.bn_aggr(mv[:, b, :], st[:, b, :])
                step(last)
                asks(ts(c[0].rearrange("p (b o) -> p b o", o=1), mv[:, :, 1:2], LN_EPS, None, ALU.add))

            def norm_scale(n):
                answered(n)
                step(V.reciprocal(c[2], c[1]))
                step(tt(c[3], c[2], c[2], ALU.mult))
                step(tt(c[3], c[3], c[0], ALU.mult))
                step(ts(c[3], c[3], -0.5, 1.5, ALU.mult, ALU.add))
                step(tt(c[2], c[2], c[3], ALU.mult))

            def norm_rows(out, src):
                for b in range(GB):
                    last = ts(out[:, b, :], src[:, b, :], mv[:, b, 0:1], c[2][:, b:b + 1], ALU.subtract, ALU.mult)
                return last

            def artanh(n, z):
                ts(c[1], z, 1.0, None, ALU.add)
                step(ts(c[2], z, -1.0, 1.0, ALU.mult, ALU.add))
                step(V.reciprocal(c[2], c[2]))
                asks(tt(c[1], c[1], c[2], ALU.mult))
                step(tt(c[5], z, z, ALU.mult))
                step(ts(c[6], c[5], 1 / 9, 1 / 7, ALU.mult, ALU.add))
                step(tt(c[6], c[6], c[5], ALU.mult))
                step(stt(c[6], c[6], 1 / 5, c[5], ALU.add, ALU.mult))
                step(stt(c[6], c[6], 1 / 3, c[5], ALU.add, ALU.mult))
                step(stt(c[6], c[6], 1.0, z, ALU.add, ALU.mult))
                step(ts(c[7], z, 0.125, None, ALU.is_lt))
                answered(n)
                step(stt(c[6], c[3], -0.5, c[6], ALU.mult, ALU.add))
                step(tt(c[6], c[6], c[7], ALU.mult))
                step(stt(c[3], c[3], 0.5, c[6], ALU.mult, ALU.add))

            V.memset(ones, 1.0)
            dve.wait_ge(inputs_in, 16 * N_INPUTS)
            start(0)
            step(ts(epsc, epsc, 1.0, 1.0, ALU.add, ALU.add))
            step(tt(e2[:, 0, :], hb, hb, ALU.mult))
            asks(rowsum(nbsq, e2[:, 0, :]))
            answered(0)
            ts(om2, coe[:, 2:3], -1.0, 1.0, ALU.mult, ALU.add)
            ts(nc3, coe[:, 3:4], -1.0, None, ALU.mult)
            ts(oc0, coe[:, 1:2], -1.0, 1.0, ALU.mult, ALU.add)
            step(ts(kap, coe[:, 0:1], -1.0, 1.0, ALU.mult, ALU.add))
            step(tt(kap, kap, oc0, ALU.mult))
            step(tt(oc0, oc0, coe[:, 0:1], ALU.mult))
            asks(ts(nbn, nbn, MIN_NORM, None, ALU.max))
            answered(1)
            ts(nbt, nbt, MAX_NORM, None, ALU.min)
            step(V.reciprocal(nbn, nbn))
            tt(y2, nbt, nbt, ALU.mult)
            step(tt(nbn, nbn, nbt, ALU.mult))
            step(ts(hb, hb, nbn, None, ALU.mult))
            V.memset(pair, 0.0).then_inc(setup_done, 1)
            assert count[0] == SETUP_STEPS, count

            def l0_rows(g, first=False):
                start(g * L0_STEPS + SETUP_STEPS)
                n = g * ASK0 + A_L0
                dve.wait_ge(merged, g + 1)
                step(tt(t1, blocks(rows_ps[:, :]), group(x1in, g), ALU.add))
                step(tt(t1, t1, over_features(bm), ALU.add))
                norm_stats(t1)
                norm_scale(n)
                if not first:
                    dve.wait_ge(rows_saved, g)
                    dve.wait_ge(turned, g)
                norm_rows(norm0, t1).then_inc(rows_normed, 1)
                dve.wait_ge(rows_normed, g + 1)
                dve.wait_ge(mapped_copied, g + 1)
                tt(t2, norm0, norm0, ALU.mult)
                tt(e2, mx, mx, ALU.mult)
                step(tt(e3, mx, over_features(hb), ALU.mult))
                rowsum(c[4], e3)
                rowsum(roots[:, 0:GB], t2)
                asks(rowsum(roots[:, GB:2 * GB], e2))
                answered(n + 1)
                xn, mxn = roots[:, 0:GB], roots[:, GB:2 * GB]
                step(ts(roots, roots, MIN_NORM, None, ALU.max))
                step(ts(c[0], xn, CLIP, None, ALU.min))
                artanh(n + 2, c[0])
                step(V.reciprocal(c[0], xn))
                step(tt(c[0], c[0], mxn, ALU.mult))
                asks(tt(c[0], c[0], c[3], ALU.mult))
                step(V.reciprocal(c[2], mxn))
                answered(n + 3)
                step(ts(c[1], c[1], MAX_NORM, None, ALU.min))
                tt(c[5], c[1], c[1], ALU.mult)
                step(tt(c[2], c[2], c[1], ALU.mult))
                ts(c[3], c[1], -1.0, 1.0, ALU.mult, ALU.add)
                step(tt(c[4], c[4], c[2], ALU.mult))
                step(ts(c[6], c[4], 2.0, 1.0, ALU.mult, ALU.add))
                step(stt(c[3], c[1], 1.0, c[3], ALU.add, ALU.mult))
                stt(c[7], c[6], y2, c[2], ALU.add, ALU.mult)
                step(stt(c[5], c[5], y2, c[6], ALU.mult, ALU.add))
                step(ts(c[5], c[5], MIN_NORM, None, ALU.max))
                step(V.reciprocal(roots[:, 0:GB], c[5]))
                tt(e2, mx, wide(c[7]), ALU.mult)
                step(tt(e3, over_features(hb), wide(c[3]), ALU.mult))
                step(tt(t2, e2, e3, ALU.add))
                step(tt(e2, t2, t2, ALU.mult))
                asks(rowsum(c[0], e2))
                answered(n + 4)
                step(tt(c[1], c[1], roots[:, 0:GB], ALU.mult))
                step(ts(c[4], c[1], MIN_NORM, None, ALU.max))
                step(ts(c[0], c[4], MAX_NORM, None, ALU.min))
                artanh(n + 5, c[0])
                step(V.reciprocal(c[4], c[4]))
                step(tt(c[3], c[3], c[4], ALU.mult))
                step(tt(c[3], c[3], roots[:, 0:GB], ALU.mult))
                tt(group(tangent, g), t2, wide(c[3]), ALU.mult).then_inc(tangent_made, 1)
                assert count[0] == L0_STEPS, count

            l0_rows(0, True)
            with dve.Fori(1, NG) as g:
                l0_rows(g)
            dve.wait_ge(tangent_made, NG)

            D_L1 = SETUP_STEPS + NG * L0_STEPS

            def l1_after(g, k):
                n = g * ASK1 + A_L1
                if k == 3:
                    start(g * L1_STEPS + D_L1)
                    dve.wait_ge(mapped_copied, g + (NG + 1))
                    step(tt(t2, t1, t1, ALU.mult))
                    asks(rowsum(c[0], t2))
                if k == 5:
                    answered(n)
                    step(ts(c[1], c[1], MIN_NORM, None, ALU.max))
                    step(V.reciprocal(c[2], c[1]))
                    step(stt(c[3], c[1], ARTANH_MAX, c[2], ALU.min, ALU.mult))
                    step(tt(t2, t1, wide(c[3]), ALU.mult))
                    step(ts(t2, t2, 0.0, None, ALU.max))
                    step(tt(t4, t2, t2, ALU.mult))
                    asks(rowsum(c[0], t4))
                if k == 7:
                    answered(n + 1)
                    asks(ts(c[1], c[1], MIN_NORM, None, ALU.max))
                    dve.wait_ge(ask, n + 3)
                    step(V.reciprocal(c[2], c[1]))
                if k == 9:
                    answered(n + 2)
                    step(stt(c[3], c[4], MAX_NORM, c[2], ALU.min, ALU.mult))
                    step(tt(t2, t2, wide(c[3]), ALU.mult))
                    step(tt(t2, t2, group(nodes, g), ALU.add))
                    norm_stats(t2)
                if k == 12:
                    norm_scale(n + 3)
                    x2 = group(nodes, g)
                    for b in range(GB):
                        last = ts(nodes[:, ds(4 * g + b, 1), :].rearrange("p b d -> p (b d)"), t2[:, b, :],
                                  mv[:, b, 0:1], c[2][:, b:b + 1], ALU.subtract, ALU.mult)
                    step(last)
                    tt(t2, x2, over_features(avec2[:, 0:D]), ALU.mult)
                    step(tt(t4, x2, over_features(avec2[:, D:2 * D]), ALU.mult))
                    rowsum(gcols(f1, g), t2)
                    step(rowsum(gcols(f2, g), t4))
                    assert count[0] == L1_STEPS, count

            def l1_masks(g, prev=None):
                for k in range(NC1):
                    dve.wait_ge(adj_in[k % 4], g * (16 * NC1 // 4) + 16 * (LAPS0 + k // 4 + 1))
                    ts(mask[:, k * CH1:(k + 1) * CH1, ds(g * GC, GC)], adj_ring1[:, k % 4], 0.0, None,
                       ALU.is_gt).then_inc(mask_made, 1)
                    if prev is not None:
                        l1_after(prev, k)

            l1_masks(0)
            with dve.Fori(1, NG) as g:
                l1_masks(g, g - 1)
            for k in range(NC1):
                l1_after(NG - 1, k)

            def factors(at, n, nth, feats):
                start(at)
                V.tensor_reduce(pair[:, 0:1], f2, AX, ALU.max)
                step(ts(kcol, f2, -1.0, None, ALU.mult))
                V.tensor_reduce(pair[:, 1:2], kcol, AX, ALU.max).then_inc(range_asked, 1)
                dve.wait_ge(range_known, nth)
                step(tt(half_range, pairmax[:, 0:1], pairmax[:, 1:2], ALU.add))
                step(tt(neg_mid, pairmax[:, 1:2], pairmax[:, 0:1], ALU.subtract))
                step(ts(half_range, half_range, 0.5, None, ALU.mult))
                step(ts(neg_mid, neg_mid, 0.5, None, ALU.mult))
                step(tt(beta, neg_mid, half_range, ALU.add))
                step(ts(beta, beta, -(1 - SLOPE), None, ALU.mult))
                ts(g_low, half_range, -2 * (1 - SLOPE), None, ALU.mult)
                step(ts(gcol, f1, 1 - SLOPE, beta, ALU.mult, ALU.add))
                asks(ts(gcol, gcol, g_low, 0.0, ALU.max, ALU.min))
                answered(n)

            def weights(lay, g, jb, first=False):
                n = g * NB + (lay * NG * NB + jb)
                if not (first and lay == 0 and jb < 4):
                    dve.wait_ge(w_used, n - 3)
                stt(w_ring[:, jb % 4], g_now, kcol[:, jb:jb + 1], mask[:, jb, ds(g * GC, GC)],
                    ALU.max, ALU.mult).then_inc(w_made, 1)

            def overs(g, jb):
                dve.wait_ge(w_made, g * NB + (jb + 1))
                ts(over_ring[:, jb % 4], w_ring[:, jb % 4], kcol[:, jb:jb + 1], None,
                   ALU.is_gt).then_inc(over_made, 1)

            def weigh(lay, g, prev, after, first=False):
                n = g + lay * NG
                if not (first and lay == 0):
                    dve.wait_ge(w_made, g * NB + lay * NG * NB)
                dve.wait_ge(g_fetched, n + 1)
                V.tensor_copy(g_now, g_next).then_inc(g_taken, 1)
                dve.wait_ge(g_taken, n + 1)
                for jb in range(NB):
                    weights(lay, g, jb, first)
                    if lay == 0 and jb > 0:
                        overs(g, jb - 1)
                    if prev is not None:
                        after(prev, jb)
                if lay == 0:
                    overs(g, NB - 1)

            def propagate(lay, after):
                weigh(lay, 0, None, after, first=True)
                with dve.Fori(1, NG) as g:
                    weigh(lay, g, g - 1, after)
                for jb in range(NB):
                    after(NG - 1, jb)

            D_P2 = D_L1 + NG * L1_STEPS
            factors(D_P2, A_P2, 1, nodes)
            step(tt(gsq, gcol, gcol, ALU.mult))
            sq = t1[:, 0, 0:2 * NB].rearrange("p (v b) -> p v b", v=2)
            step(tt(sq[:, 1, :], kcol, bcol, ALU.mult))
            step(tt(sq[:, 1, :], sq[:, 1, :], sq[:, 1, :], ALU.mult))
            step(tt(sq[:, 0, :], bcol, bcol, ALU.mult))
            for part in range(3):
                parts = sqs.rearrange("p b (v s) -> p v b s", v=2)[:, :, :, part]
                step(V.tensor_copy(parts, sq))
                if part < 2:
                    step(tt(sq, sq, parts, ALU.subtract))
            V.tensor_copy(y[:, :, D:D + 1], bcol.rearrange("p (b o) -> p b o", o=1))
            tt(y[:, :, 0:D], nodes, bcol.rearrange("p (b o) -> p b o", o=1).to_broadcast([P, NB, D]),
               ALU.mult).then_inc(layer_ready, 1)
            assert count[0] == P2_STEPS, count

            D_L2A = D_P2 + P2_STEPS

            def l2_first_after(g, jb):
                if jb == 6:
                    start(g * L2A_STEPS + D_L2A)
                    dve.wait_ge(sums_copied, g + (NG + 1))
                    V.tensor_reduce(q3, qsum.rearrange("p (b v s) -> p b v s", b=GB, s=3), AX, ALU.add)
                    step(V.reciprocal(c[0].rearrange("p (b o) -> p b o", o=1), num[:, :, D:D + 1]))
                    q = [q3[:, :, i:i + 1] for i in range(3)]
                    w = [a.rearrange("p (b o) -> p b o", o=1) for a in c]
                    tt(w[1], gcols(gsq, g).rearrange("p (b o) -> p b o", o=1), q[0], ALU.mult)
                    step(tt(w[2], q[2], q[1], ALU.subtract))
                    step(tt(c[1], c[1], c[2], ALU.add))
                    step(tt(c[1], c[1], c[0], ALU.mult))
                    step(stt(c[1], c[1], 0.5, c[0], ALU.mult, ALU.mult))
                    ts(c[2], c[1], -1.0, om2, ALU.mult, ALU.add)
                    step(ts(c[3], c[1], coe[:, 1:2], oc0, ALU.mult, ALU.add))
                    step(ts(c[4], c[3], nc3, coe[:, 1:2], ALU.mult, ALU.add))
                    step(tt(gcols(rgam, g), c[4], c[0], ALU.mult))
                if jb == 12:
                    step(tt(num[:, :, 0:D], num[:, :, 0:D], wide(c[0]), ALU.mult))
                    for b in range(GB):
                        last = stt(t1[:, b, :], nodes[:, ds(4 * g + b, 1), :].rearrange("p b d -> p (b d)"),
                                   c[2][:, b:b + 1], num[:, b, 0:D], ALU.mult, ALU.add)
                    step(last)
                    step(ts(t2, t1, THRESH, -THRESH, ALU.min, ALU.max))
                    step(tt(t1, t1, t2, ALU.subtract))
                if jb == 20:
                    tt(group(yfeat, g), t1, wide(gcols(bcol, g)), ALU.mult)
                    for b in range(GB):
                        last = stt(t2[:, b, :], t1[:, b, :], c[3][:, b:b + 1],
                                   nodes[:, ds(4 * g + b, 1), :].rearrange("p b d -> p (b d)"), ALU.mult, ALU.add)
                    step(last)
                    dve.wait_ge(h0_in, g * 16 + 16)
                    stt(group(nodes, g), t4, kap, t2, ALU.mult, ALU.add).then_inc(feat_done, 1)
                    assert count[0] == L2A_STEPS, count

            propagate(0, l2_first_after)

            D_L2B = D_L2A + NG * L2A_STEPS

            def l2_second_after(g, jb):
                if jb == 5:
                    start(g * L2B_STEPS + D_L2B)
                    dve.wait_ge(sums_copied, g + (2 * NG + 1))
                    step(tt(t1, num[:, :, 0:D], wide(gcols(rgam, g)), ALU.mult))
                    step(tt(t1, t1, group(nodes, g), ALU.add))
                    norm_stats(t1)
                if jb == 10:
                    norm_scale(g + A_L2B)
                    dve.wait_ge(rows_saved, g + NG)
                    dve.wait_ge(turned, g + NG)
                    norm_rows(norm2, t1).then_inc(rows_normed, 1)
                if jb == 26:
                    dve.wait_ge(mapped_copied, g + (2 * NG + 1))
                    tt(t1, t4, over_features(avec3[:, 0:D]), ALU.mult)
                    step(tt(t2, t4, over_features(avec3[:, D:2 * D]), ALU.mult))
                    rowsum(gcols(f1, g), t1)
                    step(rowsum(gcols(f2, g), t2))
                    assert count[0] == L2B_STEPS, count

            propagate(1, l2_second_after)

            D_P3 = D_L2B + NG * L2B_STEPS
            factors(D_P3, A_P3, 2, y)
            V.tensor_copy(y[:, :, D:D + 1], bcol.rearrange("p (b o) -> p b o", o=1))
            tt(y[:, :, 0:D], y[:, :, 0:D], bcol.rearrange("p (b o) -> p b o", o=1).to_broadcast([P, NB, D]),
               ALU.mult).then_inc(layer_ready, 1)
            assert count[0] == P3_STEPS, count

            D_L3 = D_P3 + P3_STEPS

            def l3_after(g, jb):
                n = g * ASK4 + A_L3
                if jb == 5:
                    start(g * L3_STEPS + D_L3)
                    dve.wait_ge(sums_copied, g + (3 * NG + 1))
                    step(V.reciprocal(c[0].rearrange("p (b o) -> p b o", o=1), num[:, :, D:D + 1]))
                    step(tt(t1, num[:, :, 0:D], wide(c[0]), ALU.mult))
                    asks(ts(t2, t1, 0.0, None, ALU.min))
                    step(ts(t1, t1, 0.0, -1.0, ALU.max, ALU.add))
                    step(tt(t1, t1, group(nodes, g), ALU.add))
                if jb == 10:
                    answered(n)
                    step(tt(t1, t1, t4, ALU.add))
                    norm_stats(t1)
                if jb == 16:
                    norm_scale(n + 1)
                    if not (isinstance(g, int) and g == 0):
                        dve.wait_ge(out_written, g * 16)
                    norm_rows(norm2, t1).then_inc(rows_normed, 1)
                    assert count[0] == L3_STEPS, count

            weigh(2, 0, None, l3_after, first=True)
            weigh(2, 1, 0, l3_after)
            with dve.Fori(2, NG) as g:
                weigh(2, g, g - 1, l3_after)
            for jb in range(NB):
                l3_after(NG - 1, jb)


INPUTS = (
    ("x", (N, D)), ("adj_t", (NG, P, NB * GC)), ("L0_gnn_x2", (N, D)), ("L0_gnn_eps1", (1,)),
    ("L0_gnn_eps2", (1,)), ("L0_gnn_W1t", (LAYERS, D, D)), ("L0_gnn_b1t", (D, LAYERS)),
    ("L0_gnn_W2t", (LAYERS, D, D)), ("L0_gnn_b2t", (D, LAYERS)), ("L0_gnn_Wmt", (2 * D, D)),
    ("L0_gnn_bm", (D,)), ("L1_gnn_weight_t", (D, D)), ("L1_gnn_bias", (D,)), ("L2_gnn_h0", (N, D)),
    ("L2_gnn_a", (2 * D, 1)), ("L2_gnn_temp", (5,)), ("L3_gnn_W", (D, D)), ("L3_gnn_a", (2 * D, 1)),
)


def kernel(x, adj, L0_gnn_x2, L0_gnn_eps1, L0_gnn_eps2, L0_gnn_W1, L0_gnn_b1, L0_gnn_W2, L0_gnn_b2, L0_gnn_Wm,
           L0_gnn_bm, L1_gnn_weight, L1_gnn_bias, L2_gnn_h0, L2_gnn_a, L2_gnn_temp, L3_gnn_W, L3_gnn_a):
    import numpy as np
    import concourse.bacc as bacc
    from concourse.bass_utils import run_bass_kernel_spmd

    adj_t = np.asarray(adj).reshape(NG, GC, NB, P).transpose(0, 3, 2, 1).reshape(NG, P, NB * GC)
    arrays = {
        "x": x, "adj_t": adj_t, "L0_gnn_x2": L0_gnn_x2, "L0_gnn_eps1": L0_gnn_eps1, "L0_gnn_eps2": L0_gnn_eps2,
        "L0_gnn_W1t": np.asarray(L0_gnn_W1).transpose(0, 2, 1), "L0_gnn_b1t": np.asarray(L0_gnn_b1).T,
        "L0_gnn_W2t": np.asarray(L0_gnn_W2).transpose(0, 2, 1), "L0_gnn_b2t": np.asarray(L0_gnn_b2).T,
        "L0_gnn_Wmt": np.asarray(L0_gnn_Wm).T, "L0_gnn_bm": L0_gnn_bm, "L1_gnn_weight_t": np.asarray(L1_gnn_weight).T,
        "L1_gnn_bias": L1_gnn_bias, "L2_gnn_h0": L2_gnn_h0, "L2_gnn_a": L2_gnn_a, "L2_gnn_temp": L2_gnn_temp,
        "L3_gnn_W": L3_gnn_W, "L3_gnn_a": L3_gnn_a,
    }
    arrays = {name: np.ascontiguousarray(a) for name, a in arrays.items()}
    nc = bacc.Bacc("TRN2", target_bir_lowering=False, num_devices=1)
    tensors = {name: nc.dram_tensor(name, shape, F32, kind="ExternalInput").ap() for name, shape in INPUTS}
    tensors["out"] = nc.dram_tensor("out", (N, D), F32, kind="ExternalOutput").ap()
    build(nc, tensors)
    r = run_bass_kernel_spmd(nc, [arrays], core_ids=[0])
    return r.results[0]["out"]
```

```python
from contextlib import ExitStack

import concourse.bass as bass
from concourse import mybir

F32 = mybir.dt.float32
BF16 = mybir.dt.bfloat16
U8 = mybir.dt.uint8
ALU = mybir.AluOpType
ACT = mybir.ActivationFunctionType
AX = mybir.AxisListType.X
ds = bass.ds

P = 128
N = 4096
D = 128
NB = N // P
NG = 8
GB = NB // NG
GC = GB * P
YW = D + 1
YS = D + 3
LAYERS = 3
PAIRS = NG // 2 - 1
LATE = NB - GB
ARENA = 53208

MIN_NORM = 1e-15
MAX_NORM = 1.0 - 1e-5
CLIP = 1.0 - 1e-7
LN_EPS = 1e-5
SLOPE = 0.2
THRESH = 1e-6
ARTANH_MAX = 6.1023553
ROW_NORM = 128.0 ** 0.5

STEPS_SETUP, STEPS_L0, STEPS_L1, STEPS_L2A, STEPS_L2B, STEPS_L3 = 8, 57, 30, 11, 9, 10
ASKS_SETUP, ASKS_L0, ASKS_L1, ASKS_L2A, ASKS_L2B, ASKS_L3 = 2, 6, 5, 1, 2, 2


def each_group(eng, body):
    body(0, 0)
    with eng.Fori(0, PAIRS) as i:
        body(i * 2 + 1, 1)
        body(i * 2 + 2, 0)
    body(NG - 1, 1)


def first(g):
    return isinstance(g, int) and g == 0


def build(nc, t):
    ctx = ExitStack()
    with ctx:
        def sem(name):
            return ctx.enter_context(nc.semaphore(name))

        arena = ctx.enter_context(nc.sbuf_tensor("arena", [P, ARENA], F32))
        used = [0]

        def take(words):
            a = used[0]
            used[0] += words
            assert used[0] <= ARENA, used
            return arena[:, a:a + words]

        def blocks(ap, w=D):
            return ap.rearrange("p (b d) -> p b d", d=w)

        mask_words = take(N * NB // 4)
        mask = mask_words.bitcast(U8).rearrange("p (b i) -> p b i", i=N)
        nodes = blocks(take(NB * D))
        y = blocks(take(NB * YS), YS)
        yfeat = tangent = blocks(take(NB * D))
        ring = take(4096)
        adj_ring1 = ring.rearrange("p (s b i) -> p s b i", s=4, i=GC)
        w_ring = ring[:, 0:4 * GC].rearrange("p (s i) -> p s i", s=4)
        edge_ring = ring[:, 3072:4096].bitcast(BF16).rearrange("p (s i) -> p s i", s=4)
        g_rows = [take(GC) for _ in range(2)]
        num_words = take(GB * YS)
        num = blocks(num_words, YS)
        t1, t2, t4 = [blocks(take(GC)) for _ in range(3)]
        ident = take(P)
        ones = take(1)
        avec2 = take(2 * D)
        w3 = take(D + 2)
        kbb = take(NB * 3 // 2).bitcast(BF16).rearrange("p (b s) -> p b s", s=3)
        bcol, kcol, kcol3, gcol, rgam = [take(NB) for _ in range(5)]
        coe = take(5)
        st = take(GB * 6).rearrange("p (b s) -> p b s", s=6)
        mv = take(GB * 2).rearrange("p (b s) -> p b s", s=2)
        c = [take(GB) for _ in range(8)]
        roots = take(2 * GB)
        qsum = take(GB * 3)
        f12 = take(2 * GB).rearrange("p (b s) -> p b s", s=2)
        squares = take(3)
        sc = take(12)
        y2, nbt, nbr, om2, oc0, kap, nc3, beta2, low2, beta3, low3, spare = [sc[:, i:i + 1] for i in range(12)]

        over = [0]

        def early(words):
            a = over[0]
            over[0] += words
            assert over[0] <= N * NB // 4
            return mask_words[:, a:a + words]

        def early_late(block, words):
            a = block * 1024 + 128
            assert words <= 896 and a >= over[0]
            return mask_words[:, a:a + words]

        early(640)
        x1in = blocks(early(NB * D))
        x2in = blocks(early(NB * D))
        adj_ring0 = early(8192).rearrange("p (s b i) -> p s b i", s=4, i=GC)
        w1t, w2t = early_late(17, LAYERS * D), early_late(18, LAYERS * D)
        wmt, whyp = early_late(19, 2 * D), early_late(20, D)
        bm, hb = early_late(21, D), early_late(22, D)
        small = early_late(23, 2 * LAYERS + 2)
        b1, b2, epsc = small[:, 0:LAYERS], small[:, LAYERS:2 * LAYERS], small[:, 2 * LAYERS:]
        ha = [early_late(24 + i, GC) for i in range(2)]
        hbb = [early_late(26 + i, GC) for i in range(2)]
        turned0 = early_late(28, GC)
        norm0, mx = blocks(early_late(29, GC)), blocks(early_late(30, GC))
        e2, e3 = blocks(g_rows[0]), blocks(num_words[:, 0:GC])
        w3t = early_late(31, D + 2)
        sums_t = num_words[:, 0:GC]
        norm2 = blocks(ring[:, 2048:2560])
        turned2 = ring[:, 2560:3072]
        N_INPUTS = 16

        def bank(name):
            return ctx.enter_context(nc.psum_tensor(name, [P, 512], F32))

        sums = [(bank("sum_a0"), bank("sum_b0")), (bank("sum_a1"), bank("sum_b1"))]
        bank4, bank5, bank6, bank7 = bank("bank4"), bank("bank5"), bank("bank6"), bank("bank7")
        mlp_a, mlp_b = bank4, bank5
        rows_ps = bank6
        turn0_ps = map0_ps = bank7
        sq_ps = (bank4, bank5)
        turn2_ps, f_ps, map2_ps = bank4, bank5, bank6
        g_ps = bank7

        x_in = [sem(f"x_in{s}") for s in range(4)]
        params_in = sem("params_in")
        adj_in = [sem(f"adj_in{s}") for s in range(4)]
        h0_in = sem("h0_in")
        out_written = sem("out_written")
        adj_used0 = sem("adj_used0")
        adj_used1 = sem("adj_used1")
        mask_made = sem("mask_made")
        ident_made = sem("ident_made")
        setup_asked = sem("setup_asked")
        setup_summed = sem("setup_summed")
        setup_done = sem("setup_done")
        sums_copied = sem("sums_copied")
        mlp_in = sem("mlp_in")
        mlp_out = sem("mlp_out")
        merged = sem("merged")
        rows_normed = sem("rows_normed")
        rows_saved = sem("rows_saved")
        turned = sem("turned")
        turned_copied = sem("turned_copied")
        mapped = sem("mapped")
        mapped_copied = sem("mapped_copied")
        ask = sem("ask")
        answer = sem("answer")
        dve_step = sem("dve_step")
        tangent_made = sem("tangent_made")
        factors_made = sem("factors_made")
        norm_asked = sem("norm_asked")
        exps_made = sem("exps_made")
        negs_made = sem("negs_made")
        feat_ready = sem("feat_ready")
        yfeat_made = sem("yfeat_made")
        h0_mixed = sem("h0_mixed")
        base_made = sem("base_made")
        pool_step = sem("pool_step")
        diag_made = sem("diag_made")
        g_spread = sem("g_spread")
        g_fetched = sem("g_fetched")
        w_made = sem("w_made")
        edge_made = sem("edge_made")
        w_used = sem("w_used")

        block = ctx.enter_context(nc.Block())

        def group(ap, g):
            return ap[:, ds(g * GB, GB), :]

        def gcols(ap, g):
            return ap[:, ds(g * GB, GB)]

        def node_block(g, b):
            return nodes[:, ds(g * GB + b, 1), :].rearrange("p b d -> p (b d)")

        def as3(col):
            return col.rearrange("p (b o) -> p b o", o=1)

        def wide(col, w=D):
            return as3(col).to_broadcast([P, GB, w])

        def flat(t3):
            return t3.rearrange("p b d -> p (b d)")

        CH0, CH1 = 4, 2
        NC0, NC1 = NB // CH0, NB // CH1
        LAPS0 = NG * NC0 // 4
        LOADS0 = NG * NC0
        L2A, L2B, L3 = 0, 1, 2
        TILES = NG * NB

        ASK_L0 = ASKS_SETUP
        ASK_L1 = ASK_L0 + NG * ASKS_L0
        ASK_L2A = ASK_L1 + NG * ASKS_L1
        ASK_L2B = ASK_L2A + NG * ASKS_L2A
        ASK_L3 = ASK_L2B + NG * ASKS_L2B

        @block.sync
        def _(sp):
            adj = t["adj_t"]

            def load0(g, k):
                src = adj[ds(g, 1), :, ds(k * CH0 * GC, CH0 * GC)].rearrange("a p n -> (a p) n")
                sp.dma_start(adj_ring0[:, k % 4].rearrange("p b i -> p (b i)"), src).then_inc(adj_in[k % 4], 16)

            def load1(g, k):
                src = adj[ds(g, 1), :, ds(k * CH1 * GC, CH1 * GC)].rearrange("a p n -> (a p) n")
                sp.dma_start(adj_ring1[:, k % 4].rearrange("p b i -> p (b i)"), src).then_inc(adj_in[k % 4], 16)

            for k in range(NC0):
                if k < 4:
                    q = slice(k * NB // 4, (k + 1) * NB // 4)
                    sp.dma_start(x1in[:, q, :], t["x"].rearrange("(b p) d -> p b d", p=P)[:, q, :]).then_inc(x_in[k], 16)
                    sp.dma_start(x2in[:, q, :], t["L0_gnn_x2"].rearrange("(b p) d -> p b d", p=P)[:, q, :]) \
                        .then_inc(x_in[k], 16)
                else:
                    sp.wait_ge(adj_used0, k - 3)
                load0(0, k)
            with sp.Fori(1, NG) as g:
                for k in range(NC0):
                    sp.wait_ge(adj_used0, g * NC0 + (k - 3))
                    load0(g, k)
            for k in range(NC1):
                if k >= 4:
                    sp.wait_ge(adj_used1, k - 3)
                    sp.wait_ge(mask_made, k - 3)
                else:
                    sp.wait_ge(adj_used0, LOADS0 - 3 + k)
                load1(0, k)
            with sp.Fori(1, NG) as g:
                for k in range(NC1):
                    chunk = g * NC1 + (k - 3)
                    sp.wait_ge(adj_used1, chunk)
                    sp.wait_ge(mask_made, chunk)
                    load1(g, k)
            h0 = t["L2_gnn_h0"].rearrange("(b p) d -> p b d", p=P)
            sp.wait_ge(factors_made, NG)
            sp.dma_start(t4, h0[:, 0:GB, :]).then_inc(h0_in, 16)
            with sp.Fori(1, NG) as g:
                sp.wait_ge(base_made, g)
                sp.dma_start(t4, group(h0, g)).then_inc(h0_in, 16)
            out = t["out"].rearrange("(b p) d -> p b d", p=P)
            with sp.Fori(0, NG) as g:
                sp.wait_ge(rows_normed, g + (2 * NG + 1))
                sp.dma_start(group(out, g), norm2).then_inc(out_written, 16)
            sp.wait_ge(out_written, 16 * NG)

        @block.gpsimd
        def _(pool):
            nc.gpsimd.memset(ident, 0.0).then_inc(ident_made, 1)
            pool.wait_ge(ident_made, 1)
            nc.gpsimd.affine_select(out=ident, in_=ident, compare_op=ALU.not_equal, fill=1.0, base=0,
                                    pattern=[[-1, P]], channel_multiplier=1).then_inc(ident_made, 1)
            pool.wait_ge(ident_made, 2)

            def diag(lay, g, parity):
                if lay != L2B:
                    pool.wait_ge(factors_made, g + (NG * lay // 2 + 1))
                if not (lay == L2A and isinstance(g, int) and g < 2):
                    pool.wait_ge(w_made, g * NB + (lay * TILES - NB))
                nc.gpsimd.tensor_tensor(blocks(g_rows[parity]),
                                        ident.rearrange("p (o d) -> p o d", o=1).to_broadcast([P, GB, D]),
                                        wide(gcols(gcol, g)), ALU.mult).then_inc(diag_made, 1)

            def l2_rows(g):
                pool.wait_ge(h0_in, g * 16 + 16)
                nc.gpsimd.tensor_tensor(flat(t4), flat(t4), kap.to_broadcast([P, GC]), ALU.mult).then_inc(pool_step, 1)
                pool.wait_ge(pool_step, g + 1)
                nc.gpsimd.tensor_tensor(t4, t4, group(nodes, g), ALU.add).then_inc(h0_mixed, 1)
                pool.wait_ge(feat_ready, g + 1)
                nc.gpsimd.tensor_tensor(group(yfeat, g), t1, wide(gcols(bcol, g)), ALU.mult).then_inc(yfeat_made, 1)

            diag(L2A, 0, 0)
            diag(L2A, 1, 1)
            with pool.Fori(0, PAIRS) as i:
                diag(L2A, i * 2 + 2, 0)
                l2_rows(i * 2)
                diag(L2A, i * 2 + 3, 1)
                l2_rows(i * 2 + 1)
            diag(L2B, 0, 0)
            l2_rows(NG - 2)
            diag(L2B, 1, 1)
            l2_rows(NG - 1)
            with pool.Fori(0, PAIRS) as i:
                diag(L2B, i * 2 + 2, 0)
                diag(L2B, i * 2 + 3, 1)
            with pool.Fori(0, PAIRS + 1) as i:
                diag(L3, i * 2, 0)
                diag(L3, i * 2 + 1, 1)

        @block.tensor
        def _(pe):
            def mm(out, w, m, start, stop, **kw):
                return nc.tensor.matmul(out, w, m, start=start, stop=stop, **kw)

            def turn(out, src):
                for b in range(GB):
                    last = nc.tensor.transpose(out[:, b * P:(b + 1) * P], src(b), ident)
                return last

            def setup(jb):
                if jb == 16:
                    pe.wait_ge(params_in, 16 * N_INPUTS)
                    mm(g_ps[:, 0:2], w3t[:, 0:D], w3t[:, D:D + 2], True, True).then_inc(setup_summed, 1)
                if jb == 20:
                    pe.wait_ge(setup_asked, 1)
                    mm(g_ps[:, 0:1], ones.to_broadcast([P, P]), t1[:, 0, 0:1], True, True).then_inc(setup_summed, 1)

            def l0_rows(g, jb):
                if jb in (1, 4, 7):
                    l = (jb - 1) // 3
                    if l == 0:
                        pe.wait_ge(sums_copied, g + 3)
                    else:
                        pe.wait_ge(mlp_in, g * 6 + 2 * l)
                    mm(mlp_a[:, :], w1t[:, l * D:(l + 1) * D], ha[l % 2], True, True)
                    mm(mlp_b[:, :], w2t[:, l * D:(l + 1) * D], hbb[l % 2], True, True).then_inc(mlp_out, 1)
                if jb == 10:
                    pe.wait_ge(mlp_in, g * 6 + 6)
                    if not first(g):
                        pe.wait_ge(rows_normed, g)
                    for b in range(GB):
                        s = slice(b * P, (b + 1) * P)
                        mm(rows_ps[:, s], ha[1][:, s], wmt[:, 0:D], True, False)
                        last = mm(rows_ps[:, s], hbb[1][:, s], wmt[:, D:2 * D], False, True)
                    last.then_inc(merged, 1)
                if jb == 15:
                    pe.wait_ge(rows_normed, g + 1)
                    if not first(g):
                        pe.wait_ge(mapped_copied, g)
                    turn(turn0_ps, lambda b: norm0[:, b, :]).then_inc(turned, 1)
                if jb == 17:
                    pe.wait_ge(turned_copied, g + 1)
                    for b in range(GB):
                        s = slice(b * P, (b + 1) * P)
                        last = mm(map0_ps[:, s], turned0[:, s], whyp, True, True)
                    last.then_inc(mapped, 1)

            def l0_sums(g, parity):
                sum_a, sum_b = sums[parity]
                pe.wait_ge(sums_copied, g + 1)
                for jb in range(NB):
                    k, q = divmod(jb, CH0)
                    if first(g) and jb % 8 == 0:
                        pe.wait_ge(x_in[jb // 8], 32)
                    if q == 0:
                        pe.wait_ge(adj_in[k % 4], g * (16 * NC0 // 4) + 16 * (k // 4 + 1))
                    mm(sum_a[:, :], x1in[:, jb, :], adj_ring0[:, k % 4, q, :], jb == 0, jb == NB - 1)
                    last = mm(sum_b[:, :], x2in[:, jb, :], adj_ring0[:, k % 4, q, :], jb == 0, jb == NB - 1)
                    if q == CH0 - 1:
                        last.then_inc(adj_used0, 1)
                    if first(g):
                        setup(jb)
                    else:
                        l0_rows(g - 1, jb)

            pe.wait_ge(ident_made, 2)
            each_group(pe, l0_sums)

            def l1_rows(g, k):
                if k == 1:
                    pe.wait_ge(sums_copied, g + (NG + 3))
                    turn(rows_ps, lambda b: sums_t[:, b * P:(b + 1) * P]).then_inc(merged, 1)

            def l1_sums(g, parity):
                sum_a = sums[parity][0]
                pe.wait_ge(sums_copied, g + (NG + 1))
                for jb in range(NB):
                    k, q = divmod(jb, CH1)
                    if first(g) and jb in (0, LATE):
                        pe.wait_ge(tangent_made, NG if jb else NG - 1)
                    if q == 0:
                        pe.wait_ge(adj_in[k % 4], g * (16 * NC1 // 4) + 16 * (LAPS0 + k // 4 + 1))
                    last = mm(sum_a[:, :], tangent[:, jb, :], adj_ring1[:, k % 4, q, :], jb == 0, jb == NB - 1)
                    if q == CH1 - 1:
                        last.then_inc(adj_used1, 1)
                    if first(g):
                        l0_rows(NG - 1, jb)
                    elif q == 1:
                        l1_rows(g - 1, k)
                    if jb == 12 and isinstance(g, int) and g == NG - 1:
                        spread(0)

            def spread(n):
                pe.wait_ge(diag_made, n + 1)
                if not first(n):
                    pe.wait_ge(g_fetched, n)
                src = g_rows[spread_parity[0]]
                spread_parity[0] ^= 1
                mm(g_ps[:, :], ones.to_broadcast([P, P]), src, True, True).then_inc(g_spread, 1)

            spread_parity = [0]

            def weigh(lay, feats, width, prev_rows, rows, late):
                def of_group(g, parity):
                    sum_ab, sq = sums[parity], sq_ps[parity]
                    pe.wait_ge(sums_copied, g + ((2 + lay) * NG + 1))
                    for jb in range(NB):
                        n = g * NB + (lay * TILES + jb)
                        s = jb % 4
                        if first(g) and jb in (0, LATE):
                            late(NG if jb else NG - 1)
                        pe.wait_ge(w_made, n + 1)
                        for b in range(GB):
                            o = (b % 2) * YS
                            last = mm(sum_ab[b // 2][:, o:o + width], w_ring[:, s, b * P:(b + 1) * P],
                                      feats[:, jb, 0:width], jb == 0 and b % 2 == 0, jb == NB - 1,
                                      skip_group_check=True)
                        if lay == L2A:
                            pe.wait_ge(edge_made, n + 1)
                            for b in range(GB):
                                last = mm(sq[:, b * 3:b * 3 + 3], edge_ring[:, s, b * P:(b + 1) * P],
                                          kbb[:, jb, :], jb == 0 and b == 0, jb == NB - 1, skip_group_check=True)
                        last.then_inc(w_used, 1)
                        if jb == 12 and not (lay == L3 and isinstance(g, int) and g == NG - 1):
                            spread(g + (lay * NG + 1))
                        if first(g):
                            prev_rows(NG - 1, jb)
                        else:
                            rows(g - 1, jb)
                each_group(pe, of_group)

            def no_rows(g, jb):
                pass

            def l1_last_rows(g, jb):
                if jb % 2:
                    l1_rows(g, jb // 2)

            def l2b_rows(g, jb):
                if jb == 14:
                    pe.wait_ge(rows_normed, g + (NG + 1))
                    turn(turn2_ps, lambda b: norm2[:, b, :]).then_inc(turned, 1)
                if jb == 17:
                    pe.wait_ge(turned_copied, g + (NG + 1))
                    pe.wait_ge(factors_made, g + NG)
                    for b in range(GB):
                        s = slice(b * P, (b + 1) * P)
                        mm(f_ps[:, 2 * b:2 * b + 2], turned2[:, s], w3[:, D:D + 2], True, True)
                        last = mm(map2_ps[:, s], turned2[:, s], w3[:, 0:D], True, True)
                    last.then_inc(mapped, 1)

            each_group(pe, l1_sums)
            weigh(L2A, y, YS, l1_last_rows, no_rows, lambda n: pe.wait_ge(factors_made, n))
            weigh(L2B, yfeat, D, no_rows, l2b_rows, lambda n: pe.wait_ge(yfeat_made, n))
            weigh(L3, y, YW, l2b_rows, no_rows, lambda n: pe.wait_ge(factors_made, NG + n))

        @block.scalar
        def _(act):
            def fn(out, in_, func, **kw):
                return nc.scalar.activation(out, in_, func, **kw)

            def on_ask(n, out, in_, func, **kw):
                act.wait_ge(ask, n + 1)
                fn(out, in_, func, **kw).then_inc(answer, 1)

            act.wait_ge(ident_made, 2)
            fn(g_rows[1][:, 0:1], ident[:, 0:1], ACT.Copy).then_inc(sums_copied, 2)
            def row(name, w=D):
                return t[name].rearrange("(a d) -> a d", a=1).to_broadcast([P, w])

            def load(dst, src):
                act.dma_start(dst, src).then_inc(params_in, 16)

            load(w1t, t["L0_gnn_W1t"].rearrange("l d e -> d l e"))
            load(w2t, t["L0_gnn_W2t"].rearrange("l d e -> d l e"))
            load(wmt, t["L0_gnn_Wmt"].rearrange("(l d) e -> d l e", l=2))
            load(whyp, t["L1_gnn_weight_t"])
            load(bm, row("L0_gnn_bm"))
            load(hb, row("L1_gnn_bias"))
            load(b1, t["L0_gnn_b1t"])
            load(b2, t["L0_gnn_b2t"])
            load(epsc[:, 0:1], row("L0_gnn_eps1", 1))
            load(epsc[:, 1:2], row("L0_gnn_eps2", 1))
            load(coe, row("L2_gnn_temp", 5))
            load(w3[:, 0:D], t["L3_gnn_W"])
            load(w3t[:, 0:D], t["L3_gnn_Wt"])
            load(w3t[:, D:D + 2], t["L3_gnn_a2"])
            load(avec2[:, 0:D], t["L2_gnn_a"][0:D].rearrange("d a -> a d").to_broadcast([P, D]))
            load(avec2[:, D:2 * D], t["L2_gnn_a"][D:2 * D].rearrange("d a -> a d").to_broadcast([P, D]))

            act.wait_ge(ask, 1)
            fn(coe, coe, ACT.Sigmoid)
            fn(squares, squares, ACT.Sqrt).then_inc(answer, 1)
            on_ask(1, nbt, squares[:, 0:1], ACT.Tanh)
            act.wait_ge(setup_done, 1)

            def l0_rows(g, parity):
                sum_a, sum_b = sums[parity]
                act.wait_ge(adj_used0, g * NC0 + NC0)
                fn(ha[0], sum_a[:, :], ACT.Copy, scale=epsc[:, 0:1])
                fn(hbb[0], sum_b[:, :], ACT.Copy, scale=epsc[:, 1:2]).then_inc(sums_copied, 1)
                for l in range(LAYERS):
                    act.wait_ge(mlp_out, g * LAYERS + (l + 1))
                    if l == 0 and not first(g):
                        act.wait_ge(merged, g)
                    fn(ha[(l + 1) % 2], mlp_a[:, :], ACT.Relu, bias=b1[:, l:l + 1]).then_inc(mlp_in, 1)
                    fn(hbb[(l + 1) % 2], mlp_b[:, :], ACT.Relu, bias=b2[:, l:l + 1]).then_inc(mlp_in, 1)
                n = g * ASKS_L0 + ASK_L0
                on_ask(n, c[1], c[0], ACT.Sqrt)
                act.wait_ge(rows_normed, g + 1)
                fn(group(nodes, g), norm0, ACT.Copy).then_inc(rows_saved, 1)
                act.wait_ge(turned, g + 1)
                fn(turned0, turn0_ps[:, :], ACT.Copy).then_inc(turned_copied, 1)
                act.wait_ge(mapped, g + 1)
                fn(flat(mx), map0_ps[:, :], ACT.Copy).then_inc(mapped_copied, 1)
                on_ask(n + 1, roots, roots, ACT.Sqrt)
                on_ask(n + 2, c[3], c[1], ACT.Ln)
                on_ask(n + 3, c[1], c[0], ACT.Tanh)
                on_ask(n + 4, c[1], c[0], ACT.Sqrt)
                on_ask(n + 5, c[3], c[1], ACT.Ln)

            each_group(act, l0_rows)

            def l1_sums_out(g, parity):
                act.wait_ge(adj_used1, g * NC1 + NC1)
                fn(sums_t, sums[parity][0][:, :], ACT.Copy).then_inc(sums_copied, 1)

            def l1_rows(g, k):
                n = g * ASKS_L1 + ASK_L1
                if k == 2:
                    act.wait_ge(merged, g + (NG + 1))
                    fn(flat(t1), rows_ps[:, :], ACT.Copy).then_inc(mapped_copied, 1)
                if k == 3:
                    on_ask(n, c[1], c[0], ACT.Sqrt)
                if k == 7:
                    on_ask(n + 1, c[1], c[0], ACT.Sqrt)
                if k == 8:
                    on_ask(n + 2, c[4], c[1], ACT.Tanh)
                if k == 9:
                    on_ask(n + 3, c[1], c[0], ACT.Sqrt)
                if k == 12:
                    act.wait_ge(ask, n + 5)
                    fn(gcols(bcol, g), c[7], ACT.Exp)
                    fn(gcols(kcol, g), c[7], ACT.Exp, scale=-(1 - SLOPE), bias=beta2)
                    fn(gcols(gcol, g), c[6], ACT.Exp).then_inc(answer, 1)

            def l1_group(g, parity):
                if not first(g):
                    for k in range(NC1):
                        l1_rows(g - 1, k)
                l1_sums_out(g, parity)

            def fetch_g(n, parity):
                act.wait_ge(g_spread, n + 1)
                fn(g_rows[parity], g_ps[:, :], ACT.Copy).then_inc(g_fetched, 1)

            def sums_ready(lay, g):
                act.wait_ge(w_used, g * NB + (lay * TILES + NB))

            def copy_num(parity, width):
                for half, ps in enumerate(sums[parity]):
                    last = fn(num[:, 2 * half:2 * half + 2, 0:width], blocks(ps[:, 0:2 * YS], YS)[:, :, 0:width], ACT.Copy)
                return last

            def l2a_group(g, parity):
                for jb in range(NB):
                    n = g * NB + jb
                    act.wait_ge(w_made, n + 1)
                    if not first(g) or jb >= 4:
                        act.wait_ge(w_used, n - 3)
                    fn(edge_ring[:, jb % 4], w_ring[:, jb % 4], ACT.Sign).then_inc(edge_made, 1)
                    if jb == 16:
                        fetch_g(g + 1, parity ^ 1)
                    if first(g):
                        if jb % 2:
                            l1_rows(NG - 1, jb // 2)
                    else:
                        l2a_rows(g - 1, jb)
                sums_ready(L2A, g)
                if not first(g):
                    act.wait_ge(feat_ready, g)
                copy_num(parity, YS)
                fn(qsum, sq_ps[parity][:, 0:GB * 3], ACT.Copy).then_inc(sums_copied, 1)

            def l2a_rows(g, jb):
                if jb == 7:
                    act.wait_ge(ask, g * ASKS_L2A + (ASK_L2A + 1))
                    for b in range(GB):
                        last = fn(num[:, b, 0:D], num[:, b, 0:D], ACT.Copy, scale=c[0][:, b:b + 1])
                    last.then_inc(answer, 1)

            def l2b_rows(g, jb):
                n = g * ASKS_L2B + ASK_L2B
                if jb == 5:
                    on_ask(n, c[1], c[0], ACT.Sqrt)
                if jb == 9:
                    act.wait_ge(norm_asked, g + 1)
                    if not first(g):
                        act.wait_ge(turned, g + NG)
                    normalize()
                    act.wait_ge(rows_normed, g + (NG + 1))
                    fn(group(nodes, g), norm2, ACT.Copy).then_inc(rows_saved, 1)
                if jb == 15:
                    act.wait_ge(turned, g + (NG + 1))
                    fn(turned2, turn2_ps[:, :], ACT.Copy).then_inc(turned_copied, 1)
                if jb == 18:
                    act.wait_ge(mapped, g + (NG + 1))
                    fn(f12.rearrange("p b s -> p (b s)"), f_ps[:, 0:2 * GB], ACT.Copy).then_inc(mapped_copied, 1)
                if jb == 22:
                    act.wait_ge(ask, n + 2)
                    fn(gcols(bcol, g), f12[:, :, 1:2].rearrange("p b s -> p (b s)"), ACT.Exp)
                    fn(gcols(kcol3, g), f12[:, :, 1:2].rearrange("p b s -> p (b s)"), ACT.Exp,
                       scale=-(1 - SLOPE), bias=beta3)
                    fn(gcols(gcol, g), c[6], ACT.Exp).then_inc(exps_made, 1)
                    act.wait_ge(exps_made, g + 1)
                    fn(y[:, ds(g * GB, GB), D:D + 1], as3(gcols(bcol, g)), ACT.Copy).then_inc(answer, 1)
                    for b in range(GB):
                        last = fn(y[:, ds(g * GB + b, 1), 0:D].rearrange("p b d -> p (b d)"),
                                  map2_ps[:, b * P:(b + 1) * P], ACT.Copy, scale=bcol[:, ds(g * GB + b, 1)])
                    last.then_inc(factors_made, 1)

            def normalize():
                for b in range(GB):
                    last = fn(norm2[:, b, :], t1[:, b, :], ACT.Identity, scale=c[2][:, b:b + 1], bias=c[4][:, b:b + 1])
                last.then_inc(rows_normed, 1)

            def l2b_group(g, parity):
                for jb in range(NB):
                    if first(g):
                        l2a_rows(NG - 1, jb)
                    else:
                        l2b_rows(g - 1, jb)
                    if jb == 12:
                        fetch_g(g + (NG + 1), parity ^ 1)
                sums_ready(L2B, g)
                if first(g):
                    act.wait_ge(base_made, NG)
                    act.wait_ge(yfeat_made, NG)
                else:
                    act.wait_ge(rows_normed, g + NG)
                for b in range(GB):
                    o = (b % 2) * YS
                    last = fn(t1[:, b, :], sums[parity][b // 2][:, o:o + D], ACT.Copy,
                              scale=rgam[:, ds(g * GB + b, 1)])
                last.then_inc(sums_copied, 1)

            def l3_rows(g, jb):
                n = g * ASKS_L3 + ASK_L3
                if jb == 5:
                    act.wait_ge(ask, n + 1)
                    for b in range(GB):
                        last = fn(t2[:, b, :], num[:, b, 0:D], ACT.Relu, scale=c[5][:, b:b + 1])
                    last.then_inc(negs_made, 1)
                    for b in range(GB):
                        fn(t1[:, b, :], num[:, b, 0:D], ACT.Relu, scale=c[0][:, b:b + 1])
                    act.wait_ge(negs_made, g + 1)
                    fn(flat(t4), flat(t2), ACT.Exp, scale=-1.0).then_inc(answer, 1)
                if jb == 9:
                    on_ask(n + 1, c[1], c[0], ACT.Sqrt)
                if jb == 14:
                    act.wait_ge(norm_asked, g + (NG + 1))
                    if not first(g):
                        act.wait_ge(out_written, g * 16)
                    normalize()

            def l3_group(g, parity):
                for jb in range(NB):
                    if first(g):
                        l2b_rows(NG - 1, jb)
                    else:
                        l3_rows(g - 1, jb)
                    if jb == 12 and not (isinstance(g, int) and g == NG - 1):
                        fetch_g(g + (2 * NG + 1), parity ^ 1)
                sums_ready(L3, g)
                if not first(g):
                    act.wait_ge(ask, g * ASKS_L3 + ASK_L3)
                copy_num(parity, YW).then_inc(sums_copied, 1)

            each_group(act, l1_group)
            fetch_g(0, 0)
            each_group(act, l2a_group)
            each_group(act, l2b_group)
            each_group(act, l3_group)
            for jb in range(NB):
                l3_rows(NG - 1, jb)

        @block.vector
        def _(dve):
            V = nc.vector
            tt, ts, stt = V.tensor_tensor, V.tensor_scalar, V.scalar_tensor_tensor
            base, count = [0], [0]

            def step(ins):
                count[0] += 1
                ins.then_inc(dve_step, 1)
                dve.wait_ge(dve_step, base[0] + count[0])

            def start(at):
                base[0], count[0] = at, 0

            def asks(ins):
                ins.then_inc(ask, 1)

            def answered(n):
                dve.wait_ge(answer, n + 1)

            def rowsum(out, in_):
                return V.tensor_reduce(out, in_, AX, ALU.add)

            def over_features(vec):
                return vec.rearrange("p (o d) -> p o d", o=1).to_broadcast([P, GB, D])

            def norm_stats(src):
                for b in range(GB):
                    last = V.bn_stats(st[:, b, :], src[:, b, :])
                step(last)
                V.memset(spare, 0.0)
                for b in range(GB):
                    last = V.bn_aggr(mv[:, b, :], st[:, b, :])
                step(last)
                asks(ts(as3(c[0]), mv[:, :, 1:2], LN_EPS, None, ALU.add))

            def norm_scale(n):
                answered(n)
                step(V.reciprocal(c[2], c[1]))
                step(tt(c[3], c[2], c[2], ALU.mult))
                step(tt(c[3], c[3], c[0], ALU.mult))
                step(ts(c[3], c[3], -0.5, 1.5, ALU.mult, ALU.add))
                step(tt(c[2], c[2], c[3], ALU.mult))

            def norm_for_act(n):
                norm_scale(n)
                stt(as3(c[4]), mv[:, :, 0:1], -1.0, as3(c[2]), ALU.mult, ALU.mult).then_inc(norm_asked, 1)

            def artanh_ask(z):
                ts(c[1], z, 1.0, None, ALU.add)
                step(ts(c[2], z, -1.0, 1.0, ALU.mult, ALU.add))
                step(V.reciprocal(c[2], c[2]))
                asks(tt(c[1], c[1], c[2], ALU.mult))
                step(tt(c[5], z, z, ALU.mult))
                step(ts(c[6], c[5], 1 / 9, 1 / 7, ALU.mult, ALU.add))
                step(tt(c[6], c[6], c[5], ALU.mult))
                step(stt(c[6], c[6], 1 / 5, c[5], ALU.add, ALU.mult))
                step(stt(c[6], c[6], 1 / 3, c[5], ALU.add, ALU.mult))
                step(stt(c[6], c[6], 1.0, z, ALU.add, ALU.mult))
                step(ts(c[7], z, 0.125, None, ALU.is_lt))

            def artanh_take(n):
                answered(n)
                step(stt(c[6], c[3], -0.5, c[6], ALU.mult, ALU.add))
                step(tt(c[6], c[6], c[7], ALU.mult))
                step(stt(c[3], c[3], 0.5, c[6], ALU.mult, ALU.add))

            V.memset(ones, 1.0)
            dve.wait_ge(params_in, 16 * N_INPUTS)
            start(0)
            ts(epsc, epsc, 1.0, 1.0, ALU.add, ALU.add)
            tt(t2[:, 0, :], hb, hb, ALU.mult)
            step(tt(t2[:, 1, :], avec2[:, D:2 * D], avec2[:, D:2 * D], ALU.mult))
            rowsum(squares[:, 0:2], t2[:, 0:2, :])
            dve.wait_ge(setup_summed, 1)
            step(V.tensor_copy(w3[:, D:D + 2], g_ps[:, 0:2]))
            tt(t1[:, 0, 0:1], w3[:, D + 1:D + 2], w3[:, D + 1:D + 2], ALU.mult).then_inc(setup_asked, 1)
            dve.wait_ge(setup_summed, 2)
            asks(V.tensor_copy(squares[:, 2:3], g_ps[:, 0:1]))
            answered(0)
            for root, beta, low in ((1, beta2, low2), (2, beta3, low3)):
                ts(beta, squares[:, root:root + 1], -(1 - SLOPE) * ROW_NORM, None, ALU.mult)
                ts(low, squares[:, root:root + 1], -2 * (1 - SLOPE) * ROW_NORM, None, ALU.mult)
            ts(om2, coe[:, 2:3], -1.0, 1.0, ALU.mult, ALU.add)
            ts(nc3, coe[:, 3:4], -1.0, None, ALU.mult)
            ts(oc0, coe[:, 1:2], -1.0, 1.0, ALU.mult, ALU.add)
            step(ts(kap, coe[:, 0:1], -1.0, 1.0, ALU.mult, ALU.add))
            step(tt(kap, kap, oc0, ALU.mult))
            step(tt(oc0, oc0, coe[:, 0:1], ALU.mult))
            asks(ts(squares[:, 0:1], squares[:, 0:1], MIN_NORM, None, ALU.max))
            answered(1)
            ts(nbt, nbt, MAX_NORM, None, ALU.min)
            step(V.reciprocal(nbr, squares[:, 0:1]))
            tt(y2, nbt, nbt, ALU.mult)
            step(tt(nbr, nbr, nbt, ALU.mult))
            step(ts(hb, hb, nbr, None, ALU.mult))
            V.memset(spare, 0.0).then_inc(setup_done, 1)
            assert count[0] == STEPS_SETUP, count

            AT_L0 = STEPS_SETUP
            l0_parts = NC1

            def l0_rows(g, part):
                n = g * ASKS_L0 + ASK_L0
                xn, mxn, rden = roots[:, 0:GB], roots[:, GB:2 * GB], roots[:, 0:GB]
                if part == 5:
                    start(g * STEPS_L0 + AT_L0)
                    dve.wait_ge(merged, g + 1)
                    step(tt(t1, blocks(rows_ps[:, :]), group(x1in, g), ALU.add))
                    step(tt(t1, t1, over_features(bm), ALU.add))
                    norm_stats(t1)
                if part == 7:
                    norm_scale(n)
                    if not first(g):
                        dve.wait_ge(rows_saved, g)
                        dve.wait_ge(turned, g)
                    for b in range(GB):
                        last = ts(norm0[:, b, :], t1[:, b, :], mv[:, b, 0:1], c[2][:, b:b + 1],
                                  ALU.subtract, ALU.mult)
                    last.then_inc(rows_normed, 1)
                    dve.wait_ge(rows_normed, g + 1)
                    step(tt(t2, norm0, norm0, ALU.mult))
                if part == 9:
                    dve.wait_ge(mapped_copied, g + 1)
                    tt(e2, mx, mx, ALU.mult)
                    step(tt(e3, mx, over_features(hb), ALU.mult))
                    rowsum(c[4], e3)
                    rowsum(roots[:, 0:GB], t2)
                    asks(rowsum(roots[:, GB:2 * GB], e2))
                if part == 10:
                    answered(n + 1)
                    step(ts(roots, roots, MIN_NORM, None, ALU.max))
                    step(ts(c[0], xn, CLIP, None, ALU.min))
                    artanh_ask(c[0])
                if part == 11:
                    artanh_take(n + 2)
                    step(V.reciprocal(c[0], xn))
                    step(tt(c[0], c[0], mxn, ALU.mult))
                    asks(tt(c[0], c[0], c[3], ALU.mult))
                    step(V.reciprocal(c[2], mxn))
                if part == 12:
                    answered(n + 3)
                    step(ts(c[1], c[1], MAX_NORM, None, ALU.min))
                    tt(c[5], c[1], c[1], ALU.mult)
                    step(tt(c[2], c[2], c[1], ALU.mult))
                    ts(c[3], c[1], -1.0, 1.0, ALU.mult, ALU.add)
                    step(tt(c[4], c[4], c[2], ALU.mult))
                    step(ts(c[6], c[4], 2.0, 1.0, ALU.mult, ALU.add))
                    step(stt(c[3], c[1], 1.0, c[3], ALU.add, ALU.mult))
                    stt(c[7], c[6], y2, c[2], ALU.add, ALU.mult)
                    step(stt(c[5], c[5], y2, c[6], ALU.mult, ALU.add))
                    step(ts(c[5], c[5], MIN_NORM, None, ALU.max))
                    step(V.reciprocal(rden, c[5]))
                    tt(e2, mx, wide(c[7]), ALU.mult)
                    step(tt(e3, over_features(hb), wide(c[3]), ALU.mult))
                    step(tt(t2, e2, e3, ALU.add))
                    step(tt(e2, t2, t2, ALU.mult))
                    asks(rowsum(c[0], e2))
                if part == 13:
                    answered(n + 4)
                    step(tt(c[1], c[1], rden, ALU.mult))
                    step(ts(c[4], c[1], MIN_NORM, None, ALU.max))
                    step(ts(c[0], c[4], MAX_NORM, None, ALU.min))
                    artanh_ask(c[0])
                    step(V.reciprocal(c[4], c[4]))
                if part == 14:
                    artanh_take(n + 5)
                    step(tt(c[3], c[3], c[4], ALU.mult))
                    step(tt(c[3], c[3], rden, ALU.mult))
                    tt(group(tangent, g), t2, wide(c[3]), ALU.mult).then_inc(tangent_made, 1)
                    assert count[0] == STEPS_L0, count

            def l0_group(g):
                for part in range(l0_parts):
                    l0_rows(g, part)

            l0_group(0)
            with dve.Fori(1, NG - 1) as g:
                l0_group(g)

            AT_L1 = AT_L0 + NG * STEPS_L0

            def l1_rows(g, k):
                n = g * ASKS_L1 + ASK_L1
                if k == 2:
                    start(g * STEPS_L1 + AT_L1)
                    dve.wait_ge(mapped_copied, g + (NG + 1))
                    step(tt(t2, t1, t1, ALU.mult))
                    asks(rowsum(c[0], t2))
                if k == 4:
                    answered(n)
                    step(ts(c[1], c[1], MIN_NORM, None, ALU.max))
                    step(V.reciprocal(c[2], c[1]))
                    step(stt(c[3], c[1], ARTANH_MAX, c[2], ALU.min, ALU.mult))
                    step(tt(t2, t1, wide(c[3]), ALU.mult))
                if k == 5:
                    step(ts(t2, t2, 0.0, None, ALU.max))
                    step(tt(t4, t2, t2, ALU.mult))
                if k == 6:
                    asks(rowsum(c[0], t4))
                if k == 7:
                    answered(n + 1)
                    asks(ts(c[1], c[1], MIN_NORM, None, ALU.max))
                    dve.wait_ge(ask, n + 3)
                    step(V.reciprocal(c[2], c[1]))
                if k == 8:
                    answered(n + 2)
                    step(stt(c[3], c[4], MAX_NORM, c[2], ALU.min, ALU.mult))
                    step(tt(t2, t2, wide(c[3]), ALU.mult))
                    step(tt(t2, t2, group(nodes, g), ALU.add))
                if k == 9:
                    norm_stats(t2)
                if k == 10:
                    norm_scale(n + 3)
                    for b in range(GB):
                        last = ts(node_block(g, b), t2[:, b, :], mv[:, b, 0:1], c[2][:, b:b + 1],
                                  ALU.subtract, ALU.mult)
                    step(last)
                if k == 11:
                    tt(t2, group(nodes, g), over_features(avec2[:, 0:D]), ALU.mult)
                    step(tt(t4, group(nodes, g), over_features(avec2[:, D:2 * D]), ALU.mult))
                if k == 12:
                    rowsum(c[6], t2)
                    step(rowsum(c[7], t4))
                    step(ts(c[6], c[6], 1 - SLOPE, beta2, ALU.mult, ALU.add))
                    asks(ts(c[6], c[6], low2, 0.0, ALU.max, ALU.min))
                if k == 13:
                    answered(n + 4)
                    rows, b3 = ds(g * GB, GB), as3(gcols(bcol, g))
                    V.tensor_copy(y[:, rows, D:D + 1], b3)
                    step(tt(y[:, rows, D + 1:D + 2], b3, b3, ALU.mult))
                    step(tt(c[5], gcols(bcol, g), gcols(bcol, g), ALU.mult))
                    step(tt(c[5], c[5], gcols(kcol, g), ALU.mult))
                    V.tensor_copy(y[:, rows, D + 2:D + 3], as3(c[5]))
                    for part in range(3):
                        step(V.tensor_copy(kbb[:, rows, part:part + 1], as3(c[5])))
                        if part < 2:
                            step(tt(as3(c[5]), as3(c[5]), kbb[:, rows, part:part + 1], ALU.subtract))
                    tt(y[:, rows, 0:D], group(nodes, g), wide(gcols(bcol, g)), ALU.mult).then_inc(factors_made, 1)
                    assert count[0] == STEPS_L1, count

            def l1_masks(g):
                for k in range(NC1):
                    dve.wait_ge(adj_in[k % 4], g * (16 * NC1 // 4) + 16 * (LAPS0 + k // 4 + 1))
                    ts(mask[:, k * CH1:(k + 1) * CH1, ds(g * GC, GC)], adj_ring1[:, k % 4], 0.0, None,
                       ALU.is_gt).then_inc(mask_made, 1)
                    if first(g):
                        l0_rows(NG - 1, k)
                    else:
                        l1_rows(g - 1, k)

            dve.wait_ge(adj_used0, LOADS0)
            l1_masks(0)
            with dve.Fori(1, NG) as g:
                l1_masks(g)

            def weigh(lay, ks, prev_rows, rows):
                def of_group(g, parity):
                    dve.wait_ge(g_fetched, g + (lay * NG + 1))
                    for jb in range(NB):
                        n = g * NB + (lay * TILES + jb)
                        if not (first(g) and lay == L2A and jb < 4):
                            dve.wait_ge(w_used, n - 3)
                        stt(w_ring[:, jb % 4], g_rows[parity], ks[:, jb:jb + 1], mask[:, jb, ds(g * GC, GC)],
                            ALU.max, ALU.mult).then_inc(w_made, 1)
                        if first(g):
                            prev_rows(NG - 1, jb)
                        else:
                            rows(g - 1, jb)
                each_group(dve, of_group)

            AT_L2A = AT_L1 + NG * STEPS_L1
            AT_L2B = AT_L2A + NG * STEPS_L2A
            AT_L3 = AT_L2B + NG * STEPS_L2B

            def l1_last_rows(g, jb):
                if jb % 2:
                    l1_rows(g, jb // 2)

            def l2a_rows(g, jb):
                if jb == 5:
                    start(g * STEPS_L2A + AT_L2A)
                    dve.wait_ge(sums_copied, g + (2 * NG + 3))
                    step(rowsum(c[2], qsum.rearrange("p (b s) -> p b s", s=3)))
                    step(tt(as3(c[2]), num[:, :, D + 1:D + 2], as3(c[2]), ALU.subtract))
                    step(tt(c[2], c[2], gcols(gcol, g), ALU.mult))
                    step(tt(as3(c[1]), num[:, :, D + 2:D + 3], as3(c[2]), ALU.add))
                    asks(V.reciprocal(as3(c[0]), num[:, :, D:D + 1]))
                    dve.wait_ge(ask, g * ASKS_L2A + (ASK_L2A + 1))
                    step(tt(c[1], c[1], c[0], ALU.mult))
                    step(stt(c[1], c[1], 0.5, c[0], ALU.mult, ALU.mult))
                    ts(c[2], c[1], -1.0, om2, ALU.mult, ALU.add)
                    step(ts(c[3], c[1], coe[:, 1:2], oc0, ALU.mult, ALU.add))
                    step(ts(c[4], c[3], nc3, coe[:, 1:2], ALU.mult, ALU.add))
                    step(tt(gcols(rgam, g), c[4], c[0], ALU.mult))
                if jb == 10:
                    answered(g * ASKS_L2A + ASK_L2A)
                    if not first(g):
                        dve.wait_ge(yfeat_made, g)
                    for b in range(GB):
                        last = stt(t1[:, b, :], node_block(g, b), c[2][:, b:b + 1], num[:, b, 0:D], ALU.mult, ALU.add)
                    step(last)
                    step(ts(t2, t1, THRESH, -THRESH, ALU.min, ALU.max))
                    tt(t1, t1, t2, ALU.subtract).then_inc(feat_ready, 1)
                if jb == 16:
                    dve.wait_ge(feat_ready, g + 1)
                    dve.wait_ge(h0_mixed, g + 1)
                    for b in range(GB):
                        last = stt(node_block(g, b), t1[:, b, :], c[3][:, b:b + 1], t4[:, b, :], ALU.mult, ALU.add)
                    last.then_inc(base_made, 1)
                    assert count[0] == STEPS_L2A, count

            def l2b_rows(g, jb):
                n = g * ASKS_L2B + ASK_L2B
                if jb == 3:
                    start(g * STEPS_L2B + AT_L2B)
                    dve.wait_ge(sums_copied, g + (3 * NG + 3))
                    step(tt(t1, t1, group(nodes, g), ALU.add))
                    norm_stats(t1)
                if jb == 7:
                    norm_for_act(n)
                if jb == 20:
                    dve.wait_ge(mapped_copied, g + (2 * NG + 1))
                    step(ts(as3(c[6]), f12[:, :, 0:1], 1 - SLOPE, beta3, ALU.mult, ALU.add))
                    asks(ts(c[6], c[6], low3, 0.0, ALU.max, ALU.min))
                if jb == 25:
                    answered(n + 1)
                    assert count[0] == STEPS_L2B, count

            def l3_rows(g, jb):
                n = g * ASKS_L3 + ASK_L3
                if jb == 3:
                    start(g * STEPS_L3 + AT_L3)
                    dve.wait_ge(sums_copied, g + (4 * NG + 3))
                    step(V.reciprocal(as3(c[0]), num[:, :, D:D + 1]))
                    asks(ts(c[5], c[0], -1.0, None, ALU.mult))
                if jb == 8:
                    answered(n)
                    step(stt(flat(t1), flat(t1), -1.0, flat(t4), ALU.add, ALU.add))
                    step(tt(t1, t1, group(nodes, g), ALU.add))
                    norm_stats(t1)
                if jb == 12:
                    norm_for_act(n + 1)
                    assert count[0] == STEPS_L3, count

            dve.wait_ge(adj_used1, NG * NC1)
            weigh(L2A, kcol, l1_last_rows, l2a_rows)
            weigh(L2B, kcol, l2a_rows, l2b_rows)
            weigh(L3, kcol3, l2b_rows, l3_rows)
            for jb in range(NB):
                l3_rows(NG - 1, jb)


INPUTS = (
    ("x", (N, D)), ("adj_t", (NG, P, NB * GC)), ("L0_gnn_x2", (N, D)), ("L0_gnn_eps1", (1,)),
    ("L0_gnn_eps2", (1,)), ("L0_gnn_W1t", (LAYERS, D, D)), ("L0_gnn_b1t", (D, LAYERS)),
    ("L0_gnn_W2t", (LAYERS, D, D)), ("L0_gnn_b2t", (D, LAYERS)), ("L0_gnn_Wmt", (2 * D, D)),
    ("L0_gnn_bm", (D,)), ("L1_gnn_weight_t", (D, D)), ("L1_gnn_bias", (D,)), ("L2_gnn_h0", (N, D)),
    ("L2_gnn_a", (2 * D, 1)), ("L2_gnn_temp", (5,)), ("L3_gnn_W", (D, D)), ("L3_gnn_Wt", (D, D)),
    ("L3_gnn_a2", (D, 2)),
)


def kernel(x, adj, L0_gnn_x2, L0_gnn_eps1, L0_gnn_eps2, L0_gnn_W1, L0_gnn_b1, L0_gnn_W2, L0_gnn_b2, L0_gnn_Wm,
           L0_gnn_bm, L1_gnn_weight, L1_gnn_bias, L2_gnn_h0, L2_gnn_a, L2_gnn_temp, L3_gnn_W, L3_gnn_a):
    import numpy as np
    import concourse.bacc as bacc
    from concourse.bass_utils import run_bass_kernel_spmd

    adj_t = np.asarray(adj).reshape(NG, GC, NB, P).transpose(0, 3, 2, 1).reshape(NG, P, NB * GC)
    arrays = {
        "x": x, "adj_t": adj_t, "L0_gnn_x2": L0_gnn_x2, "L0_gnn_eps1": L0_gnn_eps1, "L0_gnn_eps2": L0_gnn_eps2,
        "L0_gnn_W1t": np.asarray(L0_gnn_W1).transpose(0, 2, 1), "L0_gnn_b1t": np.asarray(L0_gnn_b1).T,
        "L0_gnn_W2t": np.asarray(L0_gnn_W2).transpose(0, 2, 1), "L0_gnn_b2t": np.asarray(L0_gnn_b2).T,
        "L0_gnn_Wmt": np.asarray(L0_gnn_Wm).T, "L0_gnn_bm": L0_gnn_bm, "L1_gnn_weight_t": np.asarray(L1_gnn_weight).T,
        "L1_gnn_bias": L1_gnn_bias, "L2_gnn_h0": L2_gnn_h0, "L2_gnn_a": L2_gnn_a, "L2_gnn_temp": L2_gnn_temp,
        "L3_gnn_W": L3_gnn_W, "L3_gnn_Wt": np.asarray(L3_gnn_W).T, "L3_gnn_a2": np.asarray(L3_gnn_a).reshape(2, D).T,
    }
    arrays = {name: np.ascontiguousarray(a) for name, a in arrays.items()}
    nc = bacc.Bacc("TRN2", target_bir_lowering=False, num_devices=1)
    tensors = {name: nc.dram_tensor(name, shape, F32, kind="ExternalInput").ap() for name, shape in INPUTS}
    tensors["out"] = nc.dram_tensor("out", (N, D), F32, kind="ExternalOutput").ap()
    build(nc, tensors)
    r = run_bass_kernel_spmd(nc, [arrays], core_ids=[0])
    return r.results[0]["out"]
```

```python
from contextlib import ExitStack

import concourse.bass as bass
from concourse import mybir

F32 = mybir.dt.float32
BF16 = mybir.dt.bfloat16
F32R = mybir.dt.float32r
U8 = mybir.dt.uint8
ALU = mybir.AluOpType
ACT = mybir.ActivationFunctionType
AX = mybir.AxisListType.X
ds = bass.ds

P = 128
N = 4096
D = 128
NB = N // P
NG = 8
GB = NB // NG
GC = GB * P
YW = D + 1
YS = D + 3
LAYERS = 3
PAIRS = NG // 2 - 1
LATE = NB - GB
ARENA = 20440
CH = 2
NC = NB // CH
PIECES = (0, 2, 4, 8, 12, 16, 20, 24, 28)
PARTS = 4 * NB * D + 8 * CH * GC

MIN_NORM = 1e-15
MAX_NORM = 1.0 - 1e-5
CLIP = 1.0 - 1e-7
LN_EPS = 1e-5
SLOPE = 0.2
THRESH = 1e-6
ARTANH_MAX = 6.1023553
ROW_NORM = 128.0 ** 0.5

STEPS_L0_NEAR = 28
STEPS_SETUP, STEPS_L0, STEPS_L1, STEPS_L2A, STEPS_L2B, STEPS_L3 = 8, 57, 30, 11, 9, 10
ASKS_SETUP, ASKS_L0, ASKS_L1, ASKS_L2A, ASKS_L2B, ASKS_L3 = 2, 6, 5, 1, 2, 2


def each_group(eng, body):
    body(0, 0)
    with eng.Fori(0, PAIRS) as i:
        body(i * 2 + 1, 1)
        body(i * 2 + 2, 0)
    body(NG - 1, 1)


def first(g):
    return isinstance(g, int) and g == 0


def build(nc, t):
    ctx = ExitStack()
    with ctx:
        def sem(name):
            return ctx.enter_context(nc.semaphore(name))

        with nc.sbuf_tensor("parts", [P, PARTS], F32R) as parts:
            pass
        mask_words = ctx.enter_context(nc.sbuf_tensor("mask_words", [P, N * NB // 4], F32))
        arena = ctx.enter_context(nc.sbuf_tensor("arena", [P, ARENA], F32))
        used = [0]

        def take(words):
            a = used[0]
            used[0] += words
            assert used[0] <= ARENA, used
            return arena[:, a:a + words]

        def blocks(ap, w=D):
            return ap.rearrange("p (b d) -> p b d", d=w)

        mask = mask_words[:, :].bitcast(U8).rearrange("p (b i) -> p b i", i=N)
        nodes = blocks(take(NB * D))
        y_words = take(NB * YS)
        y = blocks(y_words, YS)
        x1in, x2in = blocks(y_words[:, 0:NB * D]), nodes
        yfeat = tangent = blocks(take(NB * D))
        ring = take(4096)
        adj_ring = ring.rearrange("p (s b i) -> p s b i", s=4, i=GC)
        w_ring = ring[:, 0:4 * GC].rearrange("p (s i) -> p s i", s=4)
        edge_ring = ring[:, 2048:4096].bitcast(BF16).rearrange("p (s i) -> p s i", s=8)
        g_rows = [take(GC) for _ in range(2)]
        num_words = take(GB * YS)
        num = blocks(num_words, YS)
        t1, t2, t4 = [blocks(take(GC)) for _ in range(3)]
        ident = take(P)
        ones = take(1)
        warm = take(1)
        avec2 = take(2 * D)
        w3 = take(D + 2)
        kbb = take(NB * 3 // 2).bitcast(BF16).rearrange("p (b s) -> p b s", s=3)
        bcol, kcol, kcol3, gcol, rgam = [take(NB) for _ in range(5)]
        coe = take(5)
        st = take(GB * 6).rearrange("p (b s) -> p b s", s=6)
        mv = take(GB * 2).rearrange("p (b s) -> p b s", s=2)
        c = [take(GB) for _ in range(8)]
        roots = take(2 * GB)
        qsum = take(GB * 3)
        f12 = take(2 * GB).rearrange("p (b s) -> p b s", s=2)
        squares = take(3)
        sc = take(12)
        y2, nbt, nbr, om2, oc0, kap, nc3, beta2, low2, beta3, low3, spare = [sc[:, i:i + 1] for i in range(12)]

        x1_high, x1_low, x2_high, x2_low = [blocks(parts[:, i * NB * D:(i + 1) * NB * D]) for i in range(4)]
        adj_high, adj_low = [parts[:, a:a + 4 * CH * GC].rearrange("p (s b i) -> p s b i", s=4, i=GC)
                             for a in (4 * NB * D, 4 * NB * D + 4 * CH * GC)]

        def early(block, at, words):
            a = block * 1024 + 128 + at
            assert at + words <= 896 and a >= PARTS
            return mask_words[:, a:a + words]

        w1t, w2t = early(24, 0, LAYERS * D), early(24, LAYERS * D, LAYERS * D)
        small = early(24, 2 * LAYERS * D, 2 * LAYERS + 2)
        b1, b2, epsc = small[:, 0:LAYERS], small[:, LAYERS:2 * LAYERS], small[:, 2 * LAYERS:]
        wmt, whyp, bm, hb = early(25, 0, 2 * D), early(25, 2 * D, D), early(25, 3 * D, D), early(25, 4 * D, D)
        w3t = early(25, 5 * D, D + 2)
        ha = [early(26 + i, 0, GC) for i in range(2)]
        hbb = [early(28 + i, 0, GC) for i in range(2)]
        turned0, norm0 = early(30, 0, GC), blocks(early(31, 0, GC))
        mx = blocks(g_rows[1])
        e2, e3 = blocks(g_rows[0]), blocks(num_words[:, 0:GC])
        sums_t = num_words[:, 0:GC]
        norm2 = blocks(ring[:, 2048:2560])
        turned2 = ring[:, 2560:3072]
        N_INPUTS = 16

        def bank(name):
            return ctx.enter_context(nc.psum_tensor(name, [P, 512], F32))

        sums = [(bank("sum_a0"), bank("sum_b0")), (bank("sum_a1"), bank("sum_b1"))]
        bank4, bank5, bank6, bank7 = bank("bank4"), bank("bank5"), bank("bank6"), bank("bank7")
        mlp_a, mlp_b = bank4, bank5
        rows_ps = bank6
        turn0_ps = map0_ps = bank7
        sq_ps = (bank4, bank5)
        turn2_ps, map2_ps = bank4, (bank5, bank6)
        g_ps = bank7

        def map2(b):
            return map2_ps[b // 2][:, (b % 2) * (D + 2):(b % 2 + 1) * (D + 2)]

        x_in = [sem(f"x_in{s}") for s in range(len(PIECES))]
        params_in = sem("params_in")
        adj_in = [sem(f"adj_in{s}") for s in range(4)]
        h0_in = sem("h0_in")
        out_written = sem("out_written")
        x_high_made = sem("x_high_made")
        x_split = sem("x_split")
        bias_added = sem("bias_added")
        high_made = sem("high_made")
        chunk_split = sem("chunk_split")
        adj_used0 = sem("adj_used0")
        adj_used1 = sem("adj_used1")
        mask_made = sem("mask_made")
        ident_made = sem("ident_made")
        setup_asked = sem("setup_asked")
        setup_summed = sem("setup_summed")
        setup_done = sem("setup_done")
        sums_copied = sem("sums_copied")
        mlp_in = sem("mlp_in")
        mlp_out = sem("mlp_out")
        merged = sem("merged")
        rows_normed = sem("rows_normed")
        rows_saved = sem("rows_saved")
        turned = sem("turned")
        turned_copied = sem("turned_copied")
        mapped = sem("mapped")
        mapped_copied = sem("mapped_copied")
        ask = sem("ask")
        answer = sem("answer")
        dve_step = sem("dve_step")
        tangent_made = sem("tangent_made")
        columns_made = sem("columns_made")
        factors_made = sem("factors_made")
        norm_asked = sem("norm_asked")
        exps_made = sem("exps_made")
        negs_made = sem("negs_made")
        feat_ready = sem("feat_ready")
        yfeat_made = sem("yfeat_made")
        h0_mixed = sem("h0_mixed")
        base_made = sem("base_made")
        pool_step = sem("pool_step")
        diag_made = sem("diag_made")
        g_spread = sem("g_spread")
        g_fetched = sem("g_fetched")
        w_made = sem("w_made")
        edge_made = sem("edge_made")
        w_used = sem("w_used")
        edges_used = sem("edges_used")

        block = ctx.enter_context(nc.Block())

        def group(ap, g):
            return ap[:, ds(g * GB, GB), :]

        def gcols(ap, g):
            return ap[:, ds(g * GB, GB)]

        def node_block(g, b):
            return nodes[:, ds(g * GB + b, 1), :].rearrange("p b d -> p (b d)")

        def as3(col):
            return col.rearrange("p (b o) -> p b o", o=1)

        def wide(col, w=D):
            return as3(col).to_broadcast([P, GB, w])

        def flat(t3):
            return t3.rearrange("p b d -> p (b d)")

        FILLS0 = NG * NC // 4
        LOADS0 = NG * NC
        L2A, L2B, L3 = 0, 1, 2
        TILES = NG * NB

        ASK_L0 = ASKS_SETUP
        ASK_L1 = ASK_L0 + NG * ASKS_L0
        ASK_L2A = ASK_L1 + NG * ASKS_L1
        ASK_L2B = ASK_L2A + NG * ASKS_L2A
        ASK_L3 = ASK_L2B + NG * ASKS_L2B

        def piece(q):
            return slice(PIECES[q], (PIECES + (NB,))[q + 1])

        @block.sync
        def _(sp):
            adj = t["adj_t"]

            def load_chunk(g, k):
                src = adj[ds(g, 1), :, ds(k * CH * GC, CH * GC)].rearrange("a p n -> (a p) n")
                sp.dma_start(adj_ring[:, k % 4].rearrange("p b i -> p (b i)"), src).then_inc(adj_in[k % 4], 16)

            def row(name, w=D):
                return t[name].rearrange("(a d) -> a d", a=1).to_broadcast([P, w])

            def load(dst, src):
                sp.dma_start(dst, src).then_inc(params_in, 16)

            for k in range(NC):
                if k < len(PIECES):
                    for dst, name in ((x1in, "x"), (x2in, "L0_gnn_x2")):
                        q = piece(k)
                        sp.dma_start(dst[:, q, :], t[name].rearrange("(b p) d -> p b d", p=P)[:, q, :]) \
                            .then_inc(x_in[k], 16)
                if k >= 4:
                    sp.wait_ge(chunk_split, k - 3)
                load_chunk(0, k)
                if k == 3:
                    load(w1t, t["L0_gnn_W1t"].rearrange("l d e -> d l e"))
                    load(w2t, t["L0_gnn_W2t"].rearrange("l d e -> d l e"))
                    load(wmt, t["L0_gnn_Wmt"].rearrange("(l d) e -> d l e", l=2))
                    load(whyp, t["L1_gnn_weight_t"])
                if k == 4:
                    load(bm, row("L0_gnn_bm"))
                    load(hb, row("L1_gnn_bias"))
                    load(b1, t["L0_gnn_b1t"])
                    load(b2, t["L0_gnn_b2t"])
                if k == 5:
                    load(epsc[:, 0:1], row("L0_gnn_eps1", 1))
                    load(epsc[:, 1:2], row("L0_gnn_eps2", 1))
                    load(coe, row("L2_gnn_temp", 5))
                    load(w3[:, 0:D], t["L3_gnn_W"])
                if k == 6:
                    load(w3t[:, 0:D], t["L3_gnn_Wt"])
                    load(w3t[:, D:D + 2], t["L3_gnn_a2"])
                    load(avec2[:, 0:D], t["L2_gnn_a"][0:D].rearrange("d a -> a d").to_broadcast([P, D]))
                    load(avec2[:, D:2 * D], t["L2_gnn_a"][D:2 * D].rearrange("d a -> a d").to_broadcast([P, D]))
            with sp.Fori(1, NG) as g:
                for k in range(NC):
                    sp.wait_ge(chunk_split, g * NC + (k - 3))
                    load_chunk(g, k)
            for k in range(NC):
                if k >= 4:
                    sp.wait_ge(adj_used1, k - 3)
                    sp.wait_ge(mask_made, k - 3)
                else:
                    sp.wait_ge(chunk_split, LOADS0 - 3 + k)
                load_chunk(0, k)
            with sp.Fori(1, NG) as g:
                for k in range(NC):
                    chunk = g * NC + (k - 3)
                    sp.wait_ge(adj_used1, chunk)
                    sp.wait_ge(mask_made, chunk)
                    load_chunk(g, k)
            h0 = t["L2_gnn_h0"].rearrange("(b p) d -> p b d", p=P)
            sp.wait_ge(factors_made, NG)
            sp.dma_start(t4, h0[:, 0:GB, :]).then_inc(h0_in, 16)
            with sp.Fori(1, NG) as g:
                sp.wait_ge(base_made, g)
                sp.dma_start(t4, group(h0, g)).then_inc(h0_in, 16)
            out = t["out"].rearrange("(b p) d -> p b d", p=P)
            with sp.Fori(0, NG) as g:
                sp.wait_ge(rows_normed, g + (2 * NG + 1))
                sp.dma_start(group(out, g), norm2).then_inc(out_written, 16)
            sp.wait_ge(out_written, 16 * NG)

        @block.gpsimd
        def _(pool):
            nc.gpsimd.memset(ident, 0.0).then_inc(ident_made, 1)
            pool.wait_ge(ident_made, 1)
            nc.gpsimd.affine_select(out=ident, in_=ident, compare_op=ALU.not_equal, fill=1.0, base=0,
                                    pattern=[[-1, P]], channel_multiplier=1).then_inc(ident_made, 1)
            pool.wait_ge(ident_made, 2)

            pool.wait_ge(params_in, 16 * N_INPUTS)
            pool.wait_ge(x_split, len(PIECES))
            for g in range(NG):
                last = nc.gpsimd.tensor_tensor(group(x1in, g), group(x1in, g),
                                               bm.rearrange("p (o d) -> p o d", o=1).to_broadcast([P, GB, D]), ALU.add)
            last.then_inc(bias_added, 1)

            def diag(lay, g, parity):
                if lay != L2B:
                    pool.wait_ge(factors_made, g + (NG * lay // 2 + 1))
                if not (lay == L2A and isinstance(g, int) and g < 2):
                    pool.wait_ge(w_made, g * NB + (lay * TILES - NB))
                nc.gpsimd.tensor_tensor(blocks(g_rows[parity]),
                                        ident.rearrange("p (o d) -> p o d", o=1).to_broadcast([P, GB, D]),
                                        wide(gcols(gcol, g)), ALU.mult).then_inc(diag_made, 1)

            def l2_rows(g):
                pool.wait_ge(h0_in, g * 16 + 16)
                nc.gpsimd.tensor_tensor(flat(t4), flat(t4), kap.to_broadcast([P, GC]), ALU.mult).then_inc(pool_step, 1)
                pool.wait_ge(pool_step, g + 1)
                nc.gpsimd.tensor_tensor(t4, t4, group(nodes, g), ALU.add).then_inc(h0_mixed, 1)
                pool.wait_ge(feat_ready, g + 1)
                nc.gpsimd.tensor_tensor(group(yfeat, g), t1, wide(gcols(bcol, g)), ALU.mult).then_inc(yfeat_made, 1)

            diag(L2A, 0, 0)
            diag(L2A, 1, 1)
            with pool.Fori(0, PAIRS) as i:
                diag(L2A, i * 2 + 2, 0)
                l2_rows(i * 2)
                diag(L2A, i * 2 + 3, 1)
                l2_rows(i * 2 + 1)
            diag(L2B, 0, 0)
            l2_rows(NG - 2)
            diag(L2B, 1, 1)
            l2_rows(NG - 1)
            with pool.Fori(0, PAIRS) as i:
                diag(L2B, i * 2 + 2, 0)
                diag(L2B, i * 2 + 3, 1)
            with pool.Fori(0, PAIRS + 1) as i:
                diag(L3, i * 2, 0)
                diag(L3, i * 2 + 1, 1)

        @block.tensor
        def _(pe):
            def mm(out, w, m, start, stop, **kw):
                return nc.tensor.matmul(out, w, m, start=start, stop=stop, **kw)

            def turn(out, src):
                for b in range(GB):
                    last = nc.tensor.transpose(out[:, b * P:(b + 1) * P], src(b), ident)
                return last

            def setup(jb):
                if jb == 16:
                    pe.wait_ge(params_in, 16 * N_INPUTS)
                    mm(g_ps[:, 0:2], w3t[:, 0:D], w3t[:, D:D + 2], True, True).then_inc(setup_summed, 1)
                if jb == 20:
                    pe.wait_ge(setup_asked, 1)
                    mm(g_ps[:, 0:1], ones.to_broadcast([P, P]), t1[:, 0, 0:1], True, True).then_inc(setup_summed, 1)

            def l0_rows(g, stage):
                if stage < LAYERS:
                    l = stage
                    if l == 0:
                        pe.wait_ge(sums_copied, g + 3)
                    else:
                        pe.wait_ge(mlp_in, g * 6 + 2 * l)
                    mm(mlp_a[:, :], w1t[:, l * D:(l + 1) * D], ha[l % 2], True, True)
                    mm(mlp_b[:, :], w2t[:, l * D:(l + 1) * D], hbb[l % 2], True, True).then_inc(mlp_out, 1)
                if stage == 3:
                    pe.wait_ge(mlp_in, g * 6 + 6)
                    if not first(g):
                        pe.wait_ge(rows_normed, g)
                    for b in range(GB):
                        s = slice(b * P, (b + 1) * P)
                        mm(rows_ps[:, s], ha[1][:, s], wmt[:, 0:D], True, False)
                        last = mm(rows_ps[:, s], hbb[1][:, s], wmt[:, D:2 * D], False, True)
                    last.then_inc(merged, 1)
                if stage == 4:
                    pe.wait_ge(rows_normed, g + 1)
                    if not first(g):
                        pe.wait_ge(mapped_copied, g)
                    turn(turn0_ps, lambda b: norm0[:, b, :]).then_inc(turned, 1)
                if stage == 5:
                    pe.wait_ge(turned_copied, g + 1)
                    for b in range(GB):
                        s = slice(b * P, (b + 1) * P)
                        last = mm(map0_ps[:, s], turned0[:, s], whyp, True, True)
                    last.then_inc(mapped, 1)

            def l0_sums(g, parity):
                pe.wait_ge(sums_copied, g + 1)
                for jb in range(NB):
                    k, q = divmod(jb, CH)
                    if first(g) and jb in PIECES:
                        pe.wait_ge(x_split, PIECES.index(jb) + 1)
                    if q == 0:
                        pe.wait_ge(chunk_split, g * NC + (k + 1))
                    for total, high, low in zip(sums[parity], (x1_high, x2_high), (x1_low, x2_low)):
                        mm(total[:, :], high[:, jb, :], adj_low[:, k % 4, q, :], jb == 0, False)
                        mm(total[:, :], high[:, jb, :], adj_high[:, k % 4, q, :], False, False)
                        last = mm(total[:, :], low[:, jb, :], adj_high[:, k % 4, q, :], False, jb == NB - 1)
                    if q == CH - 1:
                        last.then_inc(adj_used0, 1)
                    if first(g):
                        setup(jb)
                    elif jb in L0_STAGES:
                        l0_rows(g - 1, L0_STAGES.index(jb))

            L0_STAGES, L1_STAGES = (2, 4, 6, 8, 17, 19), (1, 3, 5, 7, 14, 16)
            pe.wait_ge(ident_made, 2)
            each_group(pe, l0_sums)

            def l1_rows(g, k):
                if k == 1:
                    pe.wait_ge(sums_copied, g + (NG + 3))
                    turn(rows_ps, lambda b: sums_t[:, b * P:(b + 1) * P]).then_inc(merged, 1)

            def l1_sums(g, parity):
                sum_a = sums[parity][0]
                pe.wait_ge(sums_copied, g + (NG + 1))
                for jb in range(NB):
                    k, q = divmod(jb, CH)
                    if first(g) and jb in (0, LATE - GB, LATE):
                        pe.wait_ge(tangent_made, NG - 2 + (0, LATE - GB, LATE).index(jb))
                    if q == 0:
                        pe.wait_ge(adj_in[k % 4], g * (16 * NC // 4) + 16 * (FILLS0 + k // 4 + 1))
                    last = mm(sum_a[:, :], tangent[:, jb, :], adj_ring[:, k % 4, q, :], jb == 0, jb == NB - 1)
                    if q == CH - 1:
                        last.then_inc(adj_used1, 1)
                    if first(g) and jb in L1_STAGES:
                        l0_rows(NG - 1, L1_STAGES.index(jb))
                    elif first(g):
                        pass
                    elif q == 1:
                        l1_rows(g - 1, k)
                    if jb == 12 and isinstance(g, int) and g == NG - 1:
                        spread(0)

            def spread(n):
                pe.wait_ge(diag_made, n + 1)
                if not first(n):
                    pe.wait_ge(g_fetched, n)
                src = g_rows[spread_parity[0]]
                spread_parity[0] ^= 1
                mm(g_ps[:, :], ones.to_broadcast([P, P]), src, True, True).then_inc(g_spread, 1)

            spread_parity = [0]

            def weigh(lay, feats, width, prev_rows, rows, late):
                def of_group(g, parity):
                    sum_ab, sq = sums[parity], sq_ps[parity]
                    pe.wait_ge(sums_copied, g + ((2 + lay) * NG + 1))
                    for jb in range(NB):
                        n = g * NB + (lay * TILES + jb)
                        s = jb % 4
                        if first(g) and jb in (0, LATE):
                            late(NG if jb else NG - 1)
                        pe.wait_ge(w_made, n + 1)
                        for b in range(GB):
                            o = (b % 2) * YS
                            last = mm(sum_ab[b // 2][:, o:o + width], w_ring[:, s, b * P:(b + 1) * P],
                                      feats[:, jb, 0:width], jb == 0 and b % 2 == 0, jb == NB - 1,
                                      skip_group_check=True)
                        last.then_inc(w_used, 1)
                        if lay == L2A and jb % 4 == 3:
                            pe.wait_ge(edge_made, n + 1)
                            for e in range(jb - 3, jb + 1):
                                for b in range(GB):
                                    last = mm(sq[:, b * 3:b * 3 + 3], edge_ring[:, e % 8, b * P:(b + 1) * P],
                                              kbb[:, e, :], e == 0 and b == 0, e == NB - 1, skip_group_check=True)
                            last.then_inc(edges_used, 1)
                        if jb == 12 and not (lay == L3 and isinstance(g, int) and g == NG - 1):
                            spread(g + (lay * NG + 1))
                        if first(g):
                            prev_rows(NG - 1, jb)
                        else:
                            rows(g - 1, jb)
                each_group(pe, of_group)

            def no_rows(g, jb):
                pass

            def l1_last_rows(g, jb):
                if jb % 2:
                    l1_rows(g, jb // 2 + 1)

            def l2b_rows(g, jb):
                if jb == 16:
                    pe.wait_ge(rows_normed, g + (NG + 1))
                    turn(turn2_ps, lambda b: norm2[:, b, :]).then_inc(turned, 1)
                if jb == 20:
                    pe.wait_ge(turned_copied, g + (NG + 1))
                    pe.wait_ge(factors_made, g + NG)
                    for b in range(GB):
                        last = mm(map2(b), turned2[:, b * P:(b + 1) * P], w3, True, True)
                    last.then_inc(mapped, 1)

            each_group(pe, l1_sums)
            weigh(L2A, y, YS, l1_last_rows, no_rows, lambda n: pe.wait_ge(factors_made, n))
            weigh(L2B, yfeat, D, no_rows, l2b_rows, lambda n: pe.wait_ge(yfeat_made, n))
            weigh(L3, y, YW, l2b_rows, no_rows, lambda n: pe.wait_ge(factors_made, NG + n))

        @block.scalar
        def _(act):
            def fn(out, in_, func, **kw):
                return nc.scalar.activation(out, in_, func, **kw)

            def on_ask(n, out, in_, func, **kw):
                act.wait_ge(ask, n + 1)
                fn(out, in_, func, **kw).then_inc(answer, 1)

            act.wait_ge(ident_made, 2)
            fn(warm, ident[:, 0:1], ACT.Copy).then_inc(sums_copied, 2)
            def split_nodes(q):
                act.wait_ge(x_in[q], 32)
                q = piece(q)
                fn(x1_high[:, q, :], x1in[:, q, :], ACT.Copy)
                fn(x2_high[:, q, :], x2in[:, q, :], ACT.Copy).then_inc(x_high_made, 1)

            def l0_rows(g, parity, stage):
                sum_a, sum_b = sums[parity]
                n = g * ASKS_L0 + ASK_L0
                if stage == 0:
                    act.wait_ge(adj_used0, g * NC + NC)
                    fn(ha[0], sum_a[:, :], ACT.Copy, scale=epsc[:, 0:1])
                    fn(hbb[0], sum_b[:, :], ACT.Copy, scale=epsc[:, 1:2]).then_inc(sums_copied, 1)
                if 0 < stage <= LAYERS:
                    l = stage - 1
                    act.wait_ge(mlp_out, g * LAYERS + (l + 1))
                    if l == 0 and not first(g):
                        act.wait_ge(merged, g)
                    fn(ha[(l + 1) % 2], mlp_a[:, :], ACT.Relu, bias=b1[:, l:l + 1]).then_inc(mlp_in, 1)
                    fn(hbb[(l + 1) % 2], mlp_b[:, :], ACT.Relu, bias=b2[:, l:l + 1]).then_inc(mlp_in, 1)
                if stage == 4:
                    on_ask(n, c[1], c[0], ACT.Sqrt)
                if stage == 5:
                    act.wait_ge(rows_normed, g + 1)
                    fn(group(nodes, g), norm0, ACT.Copy).then_inc(rows_saved, 1)
                if stage == 6:
                    act.wait_ge(turned, g + 1)
                    fn(turned0, turn0_ps[:, :], ACT.Copy).then_inc(turned_copied, 1)
                if stage == 7:
                    act.wait_ge(mapped, g + 1)
                    fn(flat(mx), map0_ps[:, :], ACT.Copy).then_inc(mapped_copied, 1)
                if stage == 8:
                    on_ask(n + 1, roots, roots, ACT.Sqrt)
                if stage == 9:
                    on_ask(n + 2, c[3], c[1], ACT.Ln)
                if stage == 10:
                    on_ask(n + 3, c[1], c[0], ACT.Tanh)
                if stage == 11:
                    on_ask(n + 4, c[1], c[0], ACT.Sqrt)
                if stage == 12:
                    on_ask(n + 5, c[3], c[1], ACT.Ln)

            BEHIND = {2: 0, 3: 1, 4: 2, 5: 3, 8: 4, 10: 5, 11: 6, 12: 7, 13: 8, 14: 9, 15: 10}
            FAR_BEHIND = {4: 11, 5: 12}

            def l0_highs(g, parity):
                for k in range(NC):
                    if first(g) and k * CH in PIECES:
                        split_nodes(PIECES.index(k * CH))
                    act.wait_ge(adj_in[k % 4], g * (16 * NC // 4) + 16 * (k // 4 + 1))
                    if not (first(g) and k < 4):
                        act.wait_ge(adj_used0, g * NC + (k - 3))
                    fn(adj_high[:, k % 4], adj_ring[:, k % 4], ACT.Copy).then_inc(high_made, 1)
                    if first(g):
                        if k == 13:
                            setup()
                        continue
                    if k in BEHIND:
                        l0_rows(g - 1, parity ^ 1, BEHIND[k])
                    if k in FAR_BEHIND and not (isinstance(g, int) and g == 1):
                        l0_rows(g - 2, parity, FAR_BEHIND[k])

            def setup():
                act.wait_ge(ask, 1)
                fn(coe, coe, ACT.Sigmoid)
                fn(squares, squares, ACT.Sqrt).then_inc(answer, 1)
                on_ask(1, nbt, squares[:, 0:1], ACT.Tanh)
                act.wait_ge(setup_done, 1)

            l0_highs(0, 0)
            l0_highs(1, 1)
            with act.Fori(0, PAIRS) as i:
                l0_highs(i * 2 + 2, 0)
                l0_highs(i * 2 + 3, 1)
            for stage in range(LAYERS + 8 + 2):
                l0_rows(NG - 1, 1, stage)
                if stage in (2, 3):
                    l0_rows(NG - 2, 0, stage + 9)

            def l1_sums_out(g, parity):
                act.wait_ge(adj_used1, g * NC + NC)
                fn(sums_t, sums[parity][0][:, :], ACT.Copy).then_inc(sums_copied, 1)

            def l1_rows(g, k):
                n = g * ASKS_L1 + ASK_L1
                if k == 2:
                    act.wait_ge(merged, g + (NG + 1))
                    fn(flat(t1), rows_ps[:, :], ACT.Copy).then_inc(mapped_copied, 1)
                if k == 3:
                    on_ask(n, c[1], c[0], ACT.Sqrt)
                if k == 7:
                    on_ask(n + 1, c[1], c[0], ACT.Sqrt)
                if k == 8:
                    on_ask(n + 2, c[4], c[1], ACT.Tanh)
                if k == 9:
                    on_ask(n + 3, c[1], c[0], ACT.Sqrt)
                    fn(warm, ident[:, 0:1], ACT.Exp)
                if k == 12:
                    act.wait_ge(ask, n + 5)
                    fn(gcols(bcol, g), c[7], ACT.Exp)
                    fn(gcols(kcol, g), c[7], ACT.Exp, scale=-(1 - SLOPE), bias=beta2)
                    fn(gcols(gcol, g), c[6], ACT.Exp).then_inc(answer, 1)
                if k == 15:
                    act.wait_ge(columns_made, g + 1)
                    for b in range(GB):
                        last = fn(y[:, ds(g * GB + b, 1), 0:D].rearrange("p b d -> p (b d)"), node_block(g, b),
                                  ACT.Copy, scale=bcol[:, ds(g * GB + b, 1)])
                    last.then_inc(factors_made, 1)

            def l1_group(g, parity):
                if not first(g):
                    for k in range(NC):
                        l1_rows(g - 1, k)
                        if isinstance(g, int) and k == 13:
                            fetch_g(0, 0)
                l1_sums_out(g, parity)

            def fetch_g(n, parity):
                act.wait_ge(g_spread, n + 1)
                fn(g_rows[parity], g_ps[:, :], ACT.Copy).then_inc(g_fetched, 1)

            def sums_ready(lay, g):
                act.wait_ge(w_used, g * NB + (lay * TILES + NB))

            def copy_num(parity, width):
                for half, ps in enumerate(sums[parity]):
                    last = fn(num[:, 2 * half:2 * half + 2, 0:width], blocks(ps[:, 0:2 * YS], YS)[:, :, 0:width], ACT.Copy)
                return last

            def l2a_group(g, parity):
                for jb in range(NB):
                    n = g * NB + jb
                    act.wait_ge(w_made, n + 1)
                    if jb % 4 == 0 and not (first(g) and jb < 8):
                        act.wait_ge(edges_used, g * (NB // 4) + (jb // 4 - 1))
                    fn(edge_ring[:, jb % 8], w_ring[:, jb % 4], ACT.Sign).then_inc(edge_made, 1)
                    if jb == 16:
                        fetch_g(g + 1, parity ^ 1)
                    if first(g):
                        if jb % 2:
                            l1_rows(NG - 1, jb // 2 + 1)
                    else:
                        l2a_rows(g - 1, jb)
                sums_ready(L2A, g)
                if not first(g):
                    act.wait_ge(feat_ready, g)
                copy_num(parity, YS)
                act.wait_ge(edges_used, g * (NB // 4) + NB // 4)
                fn(qsum, sq_ps[parity][:, 0:GB * 3], ACT.Copy).then_inc(sums_copied, 1)

            def l2a_rows(g, jb):
                if jb == 7:
                    act.wait_ge(ask, g * ASKS_L2A + (ASK_L2A + 1))
                    for b in range(GB):
                        last = fn(num[:, b, 0:D], num[:, b, 0:D], ACT.Copy, scale=c[0][:, b:b + 1])
                    last.then_inc(answer, 1)

            def l2b_rows(g, jb):
                n = g * ASKS_L2B + ASK_L2B
                if jb == 10:
                    on_ask(n, c[1], c[0], ACT.Sqrt)
                if jb == 13:
                    act.wait_ge(norm_asked, g + 1)
                    if not first(g):
                        act.wait_ge(turned, g + NG)
                    normalize()
                    act.wait_ge(rows_normed, g + (NG + 1))
                    fn(group(nodes, g), norm2, ACT.Copy).then_inc(rows_saved, 1)
                if jb == 17:
                    act.wait_ge(turned, g + (NG + 1))
                    fn(turned2, turn2_ps[:, :], ACT.Copy).then_inc(turned_copied, 1)
                    fn(warm, ident[:, 0:1], ACT.Exp)
                if jb == 21:
                    act.wait_ge(mapped, g + (NG + 1))
                    for i, ps in enumerate(map2_ps):
                        last = fn(f12[:, 2 * i:2 * i + 2, :], blocks(ps[:, 0:2 * (D + 2)], D + 2)[:, :, D:D + 2], ACT.Copy)
                    last.then_inc(mapped_copied, 1)
                if jb == 25:
                    act.wait_ge(ask, n + 2)
                    fn(gcols(bcol, g), f12[:, :, 1:2].rearrange("p b s -> p (b s)"), ACT.Exp)
                    fn(gcols(kcol3, g), f12[:, :, 1:2].rearrange("p b s -> p (b s)"), ACT.Exp,
                       scale=-(1 - SLOPE), bias=beta3)
                    fn(gcols(gcol, g), c[6], ACT.Exp).then_inc(exps_made, 1)
                    act.wait_ge(exps_made, g + 1)
                    fn(y[:, ds(g * GB, GB), D:D + 1], as3(gcols(bcol, g)), ACT.Copy).then_inc(answer, 1)
                    for b in range(GB):
                        last = fn(y[:, ds(g * GB + b, 1), 0:D].rearrange("p b d -> p (b d)"),
                                  map2(b)[:, 0:D], ACT.Copy, scale=bcol[:, ds(g * GB + b, 1)])
                    last.then_inc(factors_made, 1)

            def normalize():
                for b in range(GB):
                    last = fn(norm2[:, b, :], t1[:, b, :], ACT.Identity, scale=c[2][:, b:b + 1], bias=c[4][:, b:b + 1])
                last.then_inc(rows_normed, 1)

            def l2b_group(g, parity):
                for jb in range(NB):
                    if first(g):
                        l2a_rows(NG - 1, jb)
                    else:
                        l2b_rows(g - 1, jb)
                    if jb == 12:
                        fetch_g(g + (NG + 1), parity ^ 1)
                sums_ready(L2B, g)
                if first(g):
                    act.wait_ge(base_made, NG)
                    act.wait_ge(yfeat_made, NG)
                else:
                    act.wait_ge(rows_normed, g + NG)
                for b in range(GB):
                    o = (b % 2) * YS
                    last = fn(t1[:, b, :], sums[parity][b // 2][:, o:o + D], ACT.Copy,
                              scale=rgam[:, ds(g * GB + b, 1)])
                last.then_inc(sums_copied, 1)

            def l3_rows(g, jb):
                n = g * ASKS_L3 + ASK_L3
                if jb == 5:
                    act.wait_ge(ask, n + 1)
                    for b in range(GB):
                        last = fn(t2[:, b, :], num[:, b, 0:D], ACT.Relu, scale=c[5][:, b:b + 1])
                    last.then_inc(negs_made, 1)
                    for b in range(GB):
                        fn(t1[:, b, :], num[:, b, 0:D], ACT.Relu, scale=c[0][:, b:b + 1])
                    act.wait_ge(negs_made, g + 1)
                    fn(flat(t4), flat(t2), ACT.Exp, scale=-1.0).then_inc(answer, 1)
                if jb == 18:
                    on_ask(n + 1, c[1], c[0], ACT.Sqrt)
                if jb == 22:
                    act.wait_ge(norm_asked, g + (NG + 1))
                    if not first(g):
                        act.wait_ge(out_written, g * 16)
                    normalize()

            def l3_group(g, parity):
                for jb in range(NB):
                    if first(g):
                        l2b_rows(NG - 1, jb)
                    else:
                        l3_rows(g - 1, jb)
                    if jb == 12 and not (isinstance(g, int) and g == NG - 1):
                        fetch_g(g + (2 * NG + 1), parity ^ 1)
                sums_ready(L3, g)
                if not first(g):
                    act.wait_ge(ask, g * ASKS_L3 + ASK_L3)
                copy_num(parity, YW).then_inc(sums_copied, 1)

            each_group(act, l1_group)
            each_group(act, l2a_group)
            each_group(act, l2b_group)
            each_group(act, l3_group)
            for jb in range(NB):
                l3_rows(NG - 1, jb)

        @block.vector
        def _(dve):
            V = nc.vector
            tt, ts, stt = V.tensor_tensor, V.tensor_scalar, V.scalar_tensor_tensor
            base, count = [0], [0]

            def step(ins):
                count[0] += 1
                ins.then_inc(dve_step, 1)
                dve.wait_ge(dve_step, base[0] + count[0])

            def start(at, done=0):
                base[0], count[0] = at, done

            def asks(ins):
                ins.then_inc(ask, 1)

            def answered(n):
                dve.wait_ge(answer, n + 1)

            def rowsum(out, in_):
                return V.tensor_reduce(out, in_, AX, ALU.add)

            def over_features(vec):
                return vec.rearrange("p (o d) -> p o d", o=1).to_broadcast([P, GB, D])

            def norm_moments(src):
                for b in range(GB):
                    last = V.bn_stats(st[:, b, :], src[:, b, :])
                step(last)

            def norm_ask():
                V.memset(spare, 0.0)
                for b in range(GB):
                    last = V.bn_aggr(mv[:, b, :], st[:, b, :])
                step(last)
                asks(ts(as3(c[0]), mv[:, :, 1:2], LN_EPS, None, ALU.add))

            def norm_scale(n):
                answered(n)
                step(V.reciprocal(c[2], c[1]))
                step(tt(c[3], c[2], c[2], ALU.mult))
                step(tt(c[3], c[3], c[0], ALU.mult))
                step(ts(c[3], c[3], -0.5, 1.5, ALU.mult, ALU.add))
                step(tt(c[2], c[2], c[3], ALU.mult))

            def norm_for_act(n):
                norm_scale(n)
                stt(as3(c[4]), mv[:, :, 0:1], -1.0, as3(c[2]), ALU.mult, ALU.mult).then_inc(norm_asked, 1)

            def artanh_ask(z):
                ts(c[1], z, 1.0, None, ALU.add)
                step(ts(c[2], z, -1.0, 1.0, ALU.mult, ALU.add))
                step(V.reciprocal(c[2], c[2]))
                asks(tt(c[1], c[1], c[2], ALU.mult))
                step(tt(c[5], z, z, ALU.mult))
                step(ts(c[6], c[5], 1 / 9, 1 / 7, ALU.mult, ALU.add))
                step(tt(c[6], c[6], c[5], ALU.mult))
                step(stt(c[6], c[6], 1 / 5, c[5], ALU.add, ALU.mult))
                step(stt(c[6], c[6], 1 / 3, c[5], ALU.add, ALU.mult))
                step(stt(c[6], c[6], 1.0, z, ALU.add, ALU.mult))
                step(ts(c[7], z, 0.125, None, ALU.is_lt))

            def artanh_take(n):
                answered(n)
                step(stt(c[6], c[3], -0.5, c[6], ALU.mult, ALU.add))
                step(tt(c[6], c[6], c[7], ALU.mult))
                step(stt(c[3], c[3], 0.5, c[6], ALU.mult, ALU.add))

            V.memset(ones, 1.0)

            def setup_products():
                dve.wait_ge(params_in, 16 * N_INPUTS)
                start(0)
                ts(epsc, epsc, 1.0, 1.0, ALU.add, ALU.add)
                tt(t2[:, 0, :], hb, hb, ALU.mult)
                step(tt(t2[:, 1, :], avec2[:, D:2 * D], avec2[:, D:2 * D], ALU.mult))
                rowsum(squares[:, 0:2], t2[:, 0:2, :])
                dve.wait_ge(setup_summed, 1)
                step(V.tensor_copy(w3[:, D:D + 2], g_ps[:, 0:2]))
                tt(t1[:, 0, 0:1], w3[:, D + 1:D + 2], w3[:, D + 1:D + 2], ALU.mult).then_inc(setup_asked, 1)

            def setup_rest():
                dve.wait_ge(setup_summed, 2)
                asks(V.tensor_copy(squares[:, 2:3], g_ps[:, 0:1]))
                answered(0)
                for root, beta, low in ((1, beta2, low2), (2, beta3, low3)):
                    ts(beta, squares[:, root:root + 1], -(1 - SLOPE) * ROW_NORM, None, ALU.mult)
                    ts(low, squares[:, root:root + 1], -2 * (1 - SLOPE) * ROW_NORM, None, ALU.mult)
                ts(om2, coe[:, 2:3], -1.0, 1.0, ALU.mult, ALU.add)
                ts(nc3, coe[:, 3:4], -1.0, None, ALU.mult)
                ts(oc0, coe[:, 1:2], -1.0, 1.0, ALU.mult, ALU.add)
                step(ts(kap, coe[:, 0:1], -1.0, 1.0, ALU.mult, ALU.add))
                step(tt(kap, kap, oc0, ALU.mult))
                step(tt(oc0, oc0, coe[:, 0:1], ALU.mult))
                asks(ts(squares[:, 0:1], squares[:, 0:1], MIN_NORM, None, ALU.max))
                answered(1)
                ts(nbt, nbt, MAX_NORM, None, ALU.min)
                step(V.reciprocal(nbr, squares[:, 0:1]))
                tt(y2, nbt, nbt, ALU.mult)
                step(tt(nbr, nbr, nbt, ALU.mult))
                step(ts(hb, hb, nbr, None, ALU.mult))
                V.memset(spare, 0.0).then_inc(setup_done, 1)
                assert count[0] == STEPS_SETUP, count

            AT_L0 = STEPS_SETUP

            def l0_rows(g, part):
                n = g * ASKS_L0 + ASK_L0
                xn, mxn, rden = roots[:, 0:GB], roots[:, GB:2 * GB], roots[:, 0:GB]
                if part == 5:
                    start(g * STEPS_L0 + AT_L0)
                    dve.wait_ge(merged, g + 1)
                    if first(g):
                        dve.wait_ge(bias_added, 1)
                    step(tt(t1, blocks(rows_ps[:, :]), group(x1in, g), ALU.add))
                    norm_moments(t1)
                    norm_ask()
                if part == 7:
                    norm_scale(n)
                    if not first(g):
                        dve.wait_ge(rows_saved, g)
                        dve.wait_ge(turned, g)
                    for b in range(GB):
                        last = ts(norm0[:, b, :], t1[:, b, :], mv[:, b, 0:1], c[2][:, b:b + 1],
                                  ALU.subtract, ALU.mult)
                    last.then_inc(rows_normed, 1)
                    dve.wait_ge(rows_normed, g + 1)
                    step(tt(t2, norm0, norm0, ALU.mult))
                if part == 9:
                    dve.wait_ge(mapped_copied, g + 1)
                    step(tt(e2, mx, mx, ALU.mult))
                    rowsum(roots[:, 0:GB], t2)
                    asks(rowsum(roots[:, GB:2 * GB], e2))
                if part == 10:
                    step(tt(e3, mx, over_features(hb), ALU.mult))
                    rowsum(c[4], e3)
                if part == 11:
                    answered(n + 1)
                    step(ts(roots, roots, MIN_NORM, None, ALU.max))
                    step(ts(c[0], xn, CLIP, None, ALU.min))
                    artanh_ask(c[0])
                if part == 12:
                    artanh_take(n + 2)
                    step(V.reciprocal(c[0], xn))
                    step(tt(c[0], c[0], mxn, ALU.mult))
                    asks(tt(c[0], c[0], c[3], ALU.mult))
                    step(V.reciprocal(c[2], mxn))
                    assert count[0] == STEPS_L0_NEAR, count
                if part == 13:
                    start(g * STEPS_L0 + AT_L0, STEPS_L0_NEAR)
                    answered(n + 3)
                    step(ts(c[1], c[1], MAX_NORM, None, ALU.min))
                    tt(c[5], c[1], c[1], ALU.mult)
                    step(tt(c[2], c[2], c[1], ALU.mult))
                    ts(c[3], c[1], -1.0, 1.0, ALU.mult, ALU.add)
                    step(tt(c[4], c[4], c[2], ALU.mult))
                    step(ts(c[6], c[4], 2.0, 1.0, ALU.mult, ALU.add))
                    step(stt(c[3], c[1], 1.0, c[3], ALU.add, ALU.mult))
                    stt(c[7], c[6], y2, c[2], ALU.add, ALU.mult)
                    step(stt(c[5], c[5], y2, c[6], ALU.mult, ALU.add))
                    step(ts(c[5], c[5], MIN_NORM, None, ALU.max))
                    step(V.reciprocal(rden, c[5]))
                if part == 14:
                    tt(e2, mx, wide(c[7]), ALU.mult)
                    step(tt(e3, over_features(hb), wide(c[3]), ALU.mult))
                    step(tt(t2, e2, e3, ALU.add))
                if part == 15:
                    step(tt(e2, t2, t2, ALU.mult))
                    asks(rowsum(c[0], e2))
                if part == 16:
                    answered(n + 4)
                    step(tt(c[1], c[1], rden, ALU.mult))
                    step(ts(c[4], c[1], MIN_NORM, None, ALU.max))
                    step(ts(c[0], c[4], MAX_NORM, None, ALU.min))
                    artanh_ask(c[0])
                    step(V.reciprocal(c[4], c[4]))
                if part == 17:
                    artanh_take(n + 5)
                    step(tt(c[3], c[3], c[4], ALU.mult))
                    step(tt(c[3], c[3], rden, ALU.mult))
                    tt(group(tangent, g), t2, wide(c[3]), ALU.mult).then_inc(tangent_made, 1)
                    assert count[0] == STEPS_L0, count

            def l0_lows(g):
                for k in range(NC):
                    if first(g) and k * CH in PIECES:
                        dve.wait_ge(x_high_made, PIECES.index(k * CH) + 1)
                        q = piece(PIECES.index(k * CH))
                        tt(x1_low[:, q, :], x1in[:, q, :], x1_high[:, q, :], ALU.subtract)
                        tt(x2_low[:, q, :], x2in[:, q, :], x2_high[:, q, :], ALU.subtract).then_inc(x_split, 1)
                    dve.wait_ge(high_made, g * NC + (k + 1))
                    tt(adj_low[:, k % 4], adj_ring[:, k % 4], adj_high[:, k % 4], ALU.subtract).then_inc(chunk_split, 1)
                    if first(g):
                        if k == 9:
                            setup_products()
                        if k == 12:
                            setup_rest()
                        continue
                    if k in FAR_BEHIND and not (isinstance(g, int) and g == 1):
                        l0_rows(g - 2, FAR_BEHIND[k])
                    if k in BEHIND:
                        l0_rows(g - 1, BEHIND[k])

            BEHIND = {7: 5, 8: 7, 12: 9, 13: 10, 14: 11, 15: 12}
            FAR_BEHIND = {1: 13, 2: 14, 3: 15, 5: 16, 6: 17}
            l0_lows(0)
            l0_lows(1)
            with dve.Fori(2, NG) as g:
                l0_lows(g)

            AT_L1 = AT_L0 + NG * STEPS_L0

            def l1_rows(g, k):
                n = g * ASKS_L1 + ASK_L1
                if k == 2:
                    start(g * STEPS_L1 + AT_L1)
                    dve.wait_ge(mapped_copied, g + (NG + 1))
                    step(tt(t2, t1, t1, ALU.mult))
                    asks(rowsum(c[0], t2))
                if k == 4:
                    answered(n)
                    step(ts(c[1], c[1], MIN_NORM, None, ALU.max))
                    step(V.reciprocal(c[2], c[1]))
                    step(stt(c[3], c[1], ARTANH_MAX, c[2], ALU.min, ALU.mult))
                    step(tt(t2, t1, wide(c[3]), ALU.mult))
                if k == 5:
                    step(ts(t2, t2, 0.0, None, ALU.max))
                    step(tt(t4, t2, t2, ALU.mult))
                if k == 6:
                    asks(rowsum(c[0], t4))
                if k == 7:
                    answered(n + 1)
                    asks(ts(c[1], c[1], MIN_NORM, None, ALU.max))
                    dve.wait_ge(ask, n + 3)
                    step(V.reciprocal(c[2], c[1]))
                if k == 8:
                    answered(n + 2)
                    step(stt(c[3], c[4], MAX_NORM, c[2], ALU.min, ALU.mult))
                    step(tt(t2, t2, wide(c[3]), ALU.mult))
                if k == 9:
                    step(tt(t2, t2, group(nodes, g), ALU.add))
                    norm_moments(t2)
                    norm_ask()
                if k == 10:
                    norm_scale(n + 3)
                    for b in range(GB):
                        last = ts(node_block(g, b), t2[:, b, :], mv[:, b, 0:1], c[2][:, b:b + 1],
                                  ALU.subtract, ALU.mult)
                    step(last)
                if k == 11:
                    tt(t2, group(nodes, g), over_features(avec2[:, 0:D]), ALU.mult)
                    step(tt(t4, group(nodes, g), over_features(avec2[:, D:2 * D]), ALU.mult))
                if k == 12:
                    rowsum(c[6], t2)
                    step(rowsum(c[7], t4))
                    step(ts(c[6], c[6], 1 - SLOPE, beta2, ALU.mult, ALU.add))
                    asks(ts(c[6], c[6], low2, 0.0, ALU.max, ALU.min))
                if k == 14:
                    answered(n + 4)
                    rows, b3 = ds(g * GB, GB), as3(gcols(bcol, g))
                    V.tensor_copy(y[:, rows, D:D + 1], b3)
                    step(tt(y[:, rows, D + 1:D + 2], b3, b3, ALU.mult))
                    step(tt(c[5], gcols(bcol, g), gcols(bcol, g), ALU.mult))
                    step(tt(c[5], c[5], gcols(kcol, g), ALU.mult))
                    step(V.tensor_copy(y[:, rows, D + 2:D + 3], as3(c[5])))
                if k == 15:
                    rows = ds(g * GB, GB)
                    for part in range(3):
                        last = V.tensor_copy(kbb[:, rows, part:part + 1], as3(c[5]))
                        if part < 2:
                            step(last)
                            step(tt(as3(c[5]), as3(c[5]), kbb[:, rows, part:part + 1], ALU.subtract))
                    last.then_inc(columns_made, 1)
                    assert count[0] == STEPS_L1, count

            L1_BEHIND = {5: (5,), 6: (7,), 8: (9, 10), 9: (11,), 10: (12,), 11: (13, 14, 15), 12: (16,), 13: (17,)}
            L1_FAR_BEHIND = {1: (13, 14, 15), 3: (16,), 4: (17,)}

            def l1_masks(g):
                for k in range(NC):
                    dve.wait_ge(adj_in[k % 4], g * (16 * NC // 4) + 16 * (FILLS0 + k // 4 + 1))
                    ts(mask[:, k * CH:(k + 1) * CH, ds(g * GC, GC)], adj_ring[:, k % 4], 0.0, None,
                       ALU.is_gt).then_inc(mask_made, 1)
                    if first(g):
                        for part in L1_FAR_BEHIND.get(k, ()):
                            l0_rows(NG - 2, part)
                        for part in L1_BEHIND.get(k, ()):
                            l0_rows(NG - 1, part)
                    else:
                        l1_rows(g - 1, k)

            dve.wait_ge(adj_used0, LOADS0)
            l1_masks(0)
            with dve.Fori(1, NG) as g:
                l1_masks(g)

            def weigh(lay, ks, prev_rows, rows):
                def of_group(g, parity):
                    dve.wait_ge(g_fetched, g + (lay * NG + 1))
                    for jb in range(NB):
                        n = g * NB + (lay * TILES + jb)
                        if not (first(g) and lay == L2A and jb < 4):
                            dve.wait_ge(w_used, n - 3)
                            if lay == L2A or (lay == L2B and first(g) and jb < 4):
                                dve.wait_ge(edge_made, n - 3)
                        if first(g) and lay == L2A and jb in (0, 2):
                            dve.wait_ge(adj_used1, NG * NC - 3 + jb // 2)
                        stt(w_ring[:, jb % 4], g_rows[parity], ks[:, jb:jb + 1], mask[:, jb, ds(g * GC, GC)],
                            ALU.max, ALU.mult).then_inc(w_made, 1)
                        if first(g):
                            prev_rows(NG - 1, jb)
                        else:
                            rows(g - 1, jb)
                each_group(dve, of_group)

            AT_L2A = AT_L1 + NG * STEPS_L1
            AT_L2B = AT_L2A + NG * STEPS_L2A
            AT_L3 = AT_L2B + NG * STEPS_L2B

            def l1_last_rows(g, jb):
                if jb % 2:
                    l1_rows(g, jb // 2 + 1)

            def l2a_rows(g, jb):
                if jb == 3:
                    start(g * STEPS_L2A + AT_L2A)
                    dve.wait_ge(sums_copied, g + (2 * NG + 3))
                    step(rowsum(c[2], qsum.rearrange("p (b s) -> p b s", s=3)))
                    step(tt(as3(c[2]), num[:, :, D + 1:D + 2], as3(c[2]), ALU.subtract))
                    step(tt(c[2], c[2], gcols(gcol, g), ALU.mult))
                    step(tt(as3(c[1]), num[:, :, D + 2:D + 3], as3(c[2]), ALU.add))
                    asks(V.reciprocal(as3(c[0]), num[:, :, D:D + 1]))
                if jb == 6:
                    dve.wait_ge(ask, g * ASKS_L2A + (ASK_L2A + 1))
                    step(tt(c[1], c[1], c[0], ALU.mult))
                    step(stt(c[1], c[1], 0.5, c[0], ALU.mult, ALU.mult))
                if jb == 8:
                    ts(c[2], c[1], -1.0, om2, ALU.mult, ALU.add)
                    step(ts(c[3], c[1], coe[:, 1:2], oc0, ALU.mult, ALU.add))
                    step(ts(c[4], c[3], nc3, coe[:, 1:2], ALU.mult, ALU.add))
                    step(tt(gcols(rgam, g), c[4], c[0], ALU.mult))
                if jb == 12:
                    answered(g * ASKS_L2A + ASK_L2A)
                    if not first(g):
                        dve.wait_ge(yfeat_made, g)
                    for b in range(GB):
                        last = stt(t1[:, b, :], node_block(g, b), c[2][:, b:b + 1], num[:, b, 0:D], ALU.mult, ALU.add)
                    step(last)
                if jb == 15:
                    step(ts(t2, t1, THRESH, -THRESH, ALU.min, ALU.max))
                if jb == 18:
                    tt(t1, t1, t2, ALU.subtract).then_inc(feat_ready, 1)
                if jb == 23:
                    dve.wait_ge(feat_ready, g + 1)
                    dve.wait_ge(h0_mixed, g + 1)
                    for b in range(GB):
                        last = stt(node_block(g, b), t1[:, b, :], c[3][:, b:b + 1], t4[:, b, :], ALU.mult, ALU.add)
                    last.then_inc(base_made, 1)
                    assert count[0] == STEPS_L2A, count

            def l2b_rows(g, jb):
                n = g * ASKS_L2B + ASK_L2B
                if jb == 3:
                    start(g * STEPS_L2B + AT_L2B)
                    dve.wait_ge(sums_copied, g + (3 * NG + 3))
                    step(tt(t1, t1, group(nodes, g), ALU.add))
                if jb == 6:
                    norm_moments(t1)
                if jb == 9:
                    norm_ask()
                if jb == 12:
                    norm_for_act(n)
                if jb == 23:
                    dve.wait_ge(mapped_copied, g + (2 * NG + 1))
                    step(ts(as3(c[6]), f12[:, :, 0:1], 1 - SLOPE, beta3, ALU.mult, ALU.add))
                    asks(ts(c[6], c[6], low3, 0.0, ALU.max, ALU.min))
                if jb == 27:
                    answered(n + 1)
                    assert count[0] == STEPS_L2B, count

            def l3_rows(g, jb):
                n = g * ASKS_L3 + ASK_L3
                if jb == 3:
                    start(g * STEPS_L3 + AT_L3)
                    dve.wait_ge(sums_copied, g + (4 * NG + 3))
                    step(V.reciprocal(as3(c[0]), num[:, :, D:D + 1]))
                    asks(ts(c[5], c[0], -1.0, None, ALU.mult))
                if jb == 8:
                    answered(n)
                    step(stt(flat(t1), flat(t1), -1.0, flat(t4), ALU.add, ALU.add))
                if jb == 11:
                    step(tt(t1, t1, group(nodes, g), ALU.add))
                if jb == 14:
                    norm_moments(t1)
                if jb == 17:
                    norm_ask()
                if jb == 21:
                    norm_for_act(n + 1)
                    assert count[0] == STEPS_L3, count

            weigh(L2A, kcol, l1_last_rows, l2a_rows)
            weigh(L2B, kcol, l2a_rows, l2b_rows)
            weigh(L3, kcol3, l2b_rows, l3_rows)
            for jb in range(NB):
                l3_rows(NG - 1, jb)


INPUTS = (
    ("x", (N, D)), ("adj_t", (NG, P, NB * GC)), ("L0_gnn_x2", (N, D)), ("L0_gnn_eps1", (1,)),
    ("L0_gnn_eps2", (1,)), ("L0_gnn_W1t", (LAYERS, D, D)), ("L0_gnn_b1t", (D, LAYERS)),
    ("L0_gnn_W2t", (LAYERS, D, D)), ("L0_gnn_b2t", (D, LAYERS)), ("L0_gnn_Wmt", (2 * D, D)),
    ("L0_gnn_bm", (D,)), ("L1_gnn_weight_t", (D, D)), ("L1_gnn_bias", (D,)), ("L2_gnn_h0", (N, D)),
    ("L2_gnn_a", (2 * D, 1)), ("L2_gnn_temp", (5,)), ("L3_gnn_W", (D, D)), ("L3_gnn_Wt", (D, D)),
    ("L3_gnn_a2", (D, 2)),
)


def kernel(x, adj, L0_gnn_x2, L0_gnn_eps1, L0_gnn_eps2, L0_gnn_W1, L0_gnn_b1, L0_gnn_W2, L0_gnn_b2, L0_gnn_Wm,
           L0_gnn_bm, L1_gnn_weight, L1_gnn_bias, L2_gnn_h0, L2_gnn_a, L2_gnn_temp, L3_gnn_W, L3_gnn_a):
    import numpy as np
    import concourse.bacc as bacc
    from concourse.bass_utils import run_bass_kernel_spmd

    adj_t = np.asarray(adj).reshape(NG, GC, NB, P).transpose(0, 3, 2, 1).reshape(NG, P, NB * GC)
    arrays = {
        "x": x, "adj_t": adj_t, "L0_gnn_x2": L0_gnn_x2, "L0_gnn_eps1": L0_gnn_eps1, "L0_gnn_eps2": L0_gnn_eps2,
        "L0_gnn_W1t": np.asarray(L0_gnn_W1).transpose(0, 2, 1), "L0_gnn_b1t": np.asarray(L0_gnn_b1).T,
        "L0_gnn_W2t": np.asarray(L0_gnn_W2).transpose(0, 2, 1), "L0_gnn_b2t": np.asarray(L0_gnn_b2).T,
        "L0_gnn_Wmt": np.asarray(L0_gnn_Wm).T, "L0_gnn_bm": L0_gnn_bm, "L1_gnn_weight_t": np.asarray(L1_gnn_weight).T,
        "L1_gnn_bias": L1_gnn_bias, "L2_gnn_h0": L2_gnn_h0, "L2_gnn_a": L2_gnn_a, "L2_gnn_temp": L2_gnn_temp,
        "L3_gnn_W": L3_gnn_W, "L3_gnn_Wt": np.asarray(L3_gnn_W).T, "L3_gnn_a2": np.asarray(L3_gnn_a).reshape(2, D).T,
    }
    arrays = {name: np.ascontiguousarray(a) for name, a in arrays.items()}
    nc = bacc.Bacc("TRN2", target_bir_lowering=False, num_devices=1)
    tensors = {name: nc.dram_tensor(name, shape, F32, kind="ExternalInput").ap() for name, shape in INPUTS}
    tensors["out"] = nc.dram_tensor("out", (N, D), F32, kind="ExternalOutput").ap()
    build(nc, tensors)
    r = run_bass_kernel_spmd(nc, [arrays], core_ids=[0])
    return r.results[0]["out"]
```
